# Optimizing a Trainium2 kernel written in Bass

```python
import numpy as np
import jax
import jax.numpy as jnp

def _softmax(x, axis=-1):
    return jax.nn.softmax(x, axis=axis)

def _gelu(x):
    return jax.nn.gelu(x, approximate=True)

def _silu(x):
    return jax.nn.silu(x)

def _sigmoid(x):
    return jax.nn.sigmoid(x)

def _layernorm(x, axis=-1, eps=1e-05):
    m = jnp.mean(x, axis=axis, keepdims=True)
    v = jnp.var(x, axis=axis, keepdims=True)
    return (x - m) / jnp.sqrt(v + eps)

def _scatter_add(tgt, idx, src, axis=0):
    return tgt.at[idx].add(src)

def _segment_sum(src, seg, n):
    return jax.ops.segment_sum(src, seg, n)
kernel_name = 'mk_gnn_ffn_d1_gnn_r32_2f77c2'

def setup_inputs(seed: int=0):
    np.random.seed(seed)
    _w = jnp.asarray

    def _rec_inputs():
        import jax
        import jax.numpy as jnp
        _gk = jax.random.key(seed)
        x = -0.0002117 + 1 * jax.random.normal(jax.random.fold_in(_gk, 1), (3125, 256), jnp.float32)
        _s = jax.random.randint(jax.random.fold_in(_gk, 2), (25000,), 0, 3125, jnp.int32)
        _d = jax.random.randint(jax.random.fold_in(_gk, 3), (25000,), 0, 3125, jnp.int32)
        _loop = jnp.arange(3125, dtype=jnp.int32)
        src = jnp.concatenate([_s, _d, _loop])
        dst = jnp.concatenate([_d, _s, _loop])
        _o = jnp.argsort(dst, stable=True)
        src = src[_o]
        dst = dst[_o]
        edge_weight = jax.random.uniform(jax.random.fold_in(_gk, 12), (53125,), jnp.float32, 0.0, 1)
        return (x, src, dst, edge_weight)
    x, src, dst, edge_weight = _rec_inputs()

    def _L0_gnn_setup():
        import jax, jax.numpy as jnp
        import numpy as np
        N_NODES = 3125
        N_EDGES = 100000
        D_IN = 256
        D_OUT = 256
        key = jax.random.key(seed)
        k1, k2, k3, k4, k5, k6 = jax.random.split(key, 6)
        x = jax.random.normal(k1, (N_NODES, D_IN), dtype=jnp.float32)
        edge_src = jax.random.randint(k2, (N_EDGES,), 0, N_NODES, dtype=jnp.int32)
        edge_dst = jax.random.randint(k3, (N_EDGES,), 0, N_NODES, dtype=jnp.int32)
        edge_weight = jax.random.uniform(k4, (N_EDGES,), dtype=jnp.float32)
        weight = jax.random.normal(k5, (D_IN, D_OUT), dtype=jnp.float32) * 0.02
        bias = jax.random.uniform(k6, (D_OUT,), dtype=jnp.float32)
        return {'x': x, 'edge_src': edge_src, 'edge_dst': edge_dst, 'edge_weight': edge_weight, 'weight': weight, 'bias': bias}
    _L0_gnn_all = _L0_gnn_setup()
    _L0_gnn_in = {k: v for k, v in _L0_gnn_all.items() if k in ('weight', 'bias')}
    del _L0_gnn_all

    def _L0_ffn_setup():
        import jax, jax.numpy as jnp
        import numpy as np
        TOP_K = 2
        key = jax.random.key(seed)
        ks = jax.random.split(key, 4)
        B, L, D, H, E = (8, 128, 256, 1024, 8)
        s = 0.02
        return {'x': jax.random.normal(ks[0], (B, L, D), jnp.float32), 'Wg': jax.random.normal(ks[1], (D, E), jnp.float32) * s, 'bg': jnp.zeros((E,), jnp.float32), 'W1': jax.random.normal(ks[2], (E, D, H), jnp.float32) * s, 'b1': jnp.zeros((E, H), jnp.float32), 'W2': jax.random.normal(ks[3], (E, H, D), jnp.float32) * s, 'b2': jnp.zeros((E, D), jnp.float32)}
    _L0_ffn_all = _L0_ffn_setup()
    _L0_ffn_in = {k: v for k, v in _L0_ffn_all.items() if k in ('Wg', 'bg', 'W1', 'b1', 'W2', 'b2')}
    del _L0_ffn_all
    return {'x': x, 'src': src, 'dst': dst, 'edge_weight': edge_weight, 'L0_gnn_weight': _L0_gnn_in['weight'], 'L0_gnn_bias': _L0_gnn_in['bias'], 'L0_ffn_Wg': _L0_ffn_in['Wg'], 'L0_ffn_bg': _L0_ffn_in['bg'], 'L0_ffn_W1': _L0_ffn_in['W1'], 'L0_ffn_b1': _L0_ffn_in['b1'], 'L0_ffn_W2': _L0_ffn_in['W2'], 'L0_ffn_b2': _L0_ffn_in['b2']}

def reference(x, src, dst, edge_weight, L0_gnn_weight, L0_gnn_bias, L0_ffn_Wg, L0_ffn_bg, L0_ffn_W1, L0_ffn_b1, L0_ffn_W2, L0_ffn_b2):
    import jax
    import jax.numpy as jnp

    def _L0_gnn_ref(x, edge_src, edge_dst, edge_weight, weight, bias):
        import jax, jax.numpy as jnp
        import numpy as np
        N_NODES = 3125
        N_EDGES = 100000
        D_IN = 256
        D_OUT = 256
        support = x @ weight
        msgs = support[edge_src] * edge_weight[:, None]
        out = jax.ops.segment_sum(msgs, edge_dst, num_segments=N_NODES)
        return out + bias

    def _L0_ffn_ref(x, Wg, bg, W1, b1, W2, b2):
        import jax, jax.numpy as jnp
        import numpy as np
        TOP_K = 2
        B, L, D = x.shape
        E = W1.shape[0]
        xf = x.reshape(-1, D)
        gate_logits = xf @ Wg + bg
        top_w, top_i = jax.lax.top_k(gate_logits, TOP_K)
        top_w = jax.nn.softmax(top_w, axis=-1)
        w_dense = jnp.sum(jax.nn.one_hot(top_i, E, dtype=xf.dtype) * top_w[..., None], axis=1)
        out = jnp.zeros_like(xf)
        for e in range(E):
            h = jax.nn.gelu(xf @ W1[e] + b1[e], approximate=False)
            out = out + w_dense[:, e:e + 1] * (h @ W2[e] + b2[e])
        return out.reshape(B, L, D)
    x = x + _L0_gnn_ref(_layernorm(x, axis=-1), src, dst, edge_weight, L0_gnn_weight, L0_gnn_bias)
    x = x + _L0_ffn_ref(_layernorm(x, axis=-1)[None], L0_ffn_Wg, L0_ffn_bg, L0_ffn_W1, L0_ffn_b1, L0_ffn_W2, L0_ffn_b2)[0]
    return x

_drawn_inputs = setup_inputs


def setup_inputs(seed=0):
    import zlib

    import numpy as np

    out = dict(_drawn_inputs(seed))
    spreads = {'L0_ffn_bg': (0.0, 0.1), 'L0_ffn_b1': (0.0, 0.428), 'L0_ffn_b2': (0.0, 0.1)}
    factors = {}
    for name, (base, spread) in spreads.items():
        noise = np.random.default_rng([zlib.crc32(name.encode()), seed]).standard_normal(out[name].shape)
        drawn = base * np.exp(spread * noise) if base else spread * noise
        out[name] = jnp.asarray(drawn.astype(out[name].dtype))
    for name, factor in factors.items():
        out[name] = (out[name] * factor).astype(out[name].dtype)
    return out
```

```python
import concourse.bass as bass
from concourse import mybir
from contextlib import ExitStack

PAD_ROWS = 256


class Chain:

    def __init__(self, eng, sem, base=0):
        self.eng, self.sem, self.n = eng, sem, base

    def __call__(self, ins):
        self.n = self.n + 1
        ins.then_inc(self.sem, 1)
        self.eng.wait_ge(self.sem, self.n)


def gnn_moe_layer(nc, x, src, dst, edge_w, w_gnn, b_gnn, w_gate, b_gate, w1, b1, w2, b2, out):
    f32, f32r, i32 = mybir.dt.float32, mybir.dt.float32r, mybir.dt.int32
    ACT, ALU, AX = mybir.ActivationFunctionType, mybir.AluOpType, mybir.AxisListType

    N, D = x.shape
    E = src.shape[0]
    X = w_gate.shape[1]
    H = w1.shape[2]
    KD, KH = D // 128, H // 128
    EPS = 1e-5
    NEG = -3.0e38

    P, NB, CB = 125, 25, 5
    NC = NB // CB
    LIN = 3
    assert P * NB == N
    PA = 112

    GT, WIN = 4, 64
    GE = GT * 128
    NG = -(-E // GE)
    BODY = 4
    RING = BODY * GT
    HALF = RING // 2
    NIT = NG // BODY
    assert NIT * BODY == NG and NIT >= NB
    LAST = E - (NG - 1) * GE
    NWIN = -(-N // WIN)

    T = 256
    TH = T // 128
    NT = (2 * N - X) // T + X
    NH = NT * TH
    NHP = NH + 2 * TH
    TPE = -(-N // T)
    NQ = KH // 2
    SC = 1024
    SPLITS = (KD * H + KH * D) // SC
    assert PAD_ROWS == T

    xn_d = nc.dram_tensor("xn_d", (N, D), f32, kind="Internal").ap()
    y_d = nc.dram_tensor("y_d", (N, D), f32, kind="Internal").ap()

    def by_partition(a):
        return a.rearrange("(p b) d -> p b d", b=NB)

    x_v, xn_v, y_v, out_v = by_partition(x), by_partition(xn_d), by_partition(y_d), by_partition(out[0:N, :])

    def flat(a):
        return a.rearrange("p a b -> p (a b)")

    with ExitStack() as ctx:
        def sb(name, shape, dt=f32, stack=ctx):
            return stack.enter_context(nc.sbuf_tensor(name, shape, dt))

        def pb(name, shape, stack):
            return stack.enter_context(nc.psum_tensor(name, shape, f32))

        def sem(name):
            return ctx.enter_context(nc.semaphore(name))

        ident = sb("ident", [128, 128])
        b1_in = sb("b1_in", [X * KH, 128])
        b1_t = sb("b1_t", [128, X * KH])
        b2_bc = sb("b2_bc", [128, X, D])
        w1_raw = sb("w1_raw", [128, KD, H])
        w2_raw = sb("w2_raw", [128, KH, D])
        slot_read = sb("slot_read", [128, NHP], i32)
        slot_add = sb("slot_add", [128, NHP], i32)
        slot_w = sb("slot_w", [128, NHP])
        starts = sb("starts", [1, X + 1], i32)

        def weight_parts(k, stack):
            return [sb(f"{n}_{k}", shape, f32r, stack) for n, shape in
                    (("w1_hi", [128, KD, H]), ("w1_lo", [128, KD, H]), ("w2_hi", [128, KH, D]), ("w2_lo", [128, KH, D]))]

        parts = [weight_parts(0, ctx)]

        with ExitStack() as gnn:
            def g_sb(name, shape, dt=f32):
                return sb(name, shape, dt, gnn)

            iota_w = g_sb("iota_w", [128, 128])
            iota_x = g_sb("iota_x", [128, X])
            iota_mx = g_sb("iota_mx", [128, X])
            tri = g_sb("tri", [128, 128])
            ones = g_sb("ones", [128, 128])
            zeros = g_sb("zeros", [128, PAD_ROWS // 128, D])
            thr = g_sb("thr", [128, X, TPE])
            thr_w = g_sb("thr_w", [1, NWIN])
            pad_row = g_sb("pad_row", [128, NH])
            node1 = g_sb("node1", [128, NB])
            bias_bc = g_sb("bias_bc", [128, D])
            bg_bc = g_sb("bg_bc", [128, X])
            wg_sb = g_sb("wg_sb", [128, KD, X])
            wn_sb = g_sb("wn_sb", [128, KD, D])
            x_sb = g_sb("x_sb", [P, NIT, D])
            y_sb = g_sb("y_sb", [P, NIT, D])
            bn = g_sb("bn", [P, NB, 6])
            mv = g_sb("mv", [P, NB, 2])
            ve, sq, nwt, rstd, nmr = (g_sb(n, [P, NB]) for n in ("ve", "sq", "nwt", "rstd", "nmr"))
            e_int = g_sb("e_int", [NG, 2, GE], i32)
            e_f = g_sb("e_f", [NG, 3, GE])
            base_f = g_sb("base_f", [NG, 3])
            base_r = g_sb("base_r", [1, NG])
            base_i = g_sb("base_i", [1, NG], i32)
            span = g_sb("span", [1, NWIN + 2])
            passes = g_sb("passes", [1, 1], i32)
            rel_t = g_sb("rel_t", [128, NG, GT])
            src_t = g_sb("src_t", [128, NG, GT], i32)
            ew_t = g_sb("ew_t", [128, NG, GT])
            acc = g_sb("acc", [128, KD, N + WIN])
            yt_sb = g_sb("yt_sb", [128, CB, KD, P])
            idx_ring = g_sb("idx_ring", [128, RING], i32)
            G = g_sb("G", [128, RING, D])
            S = g_sb("S", [128, RING, WIN])
            lg, lg2, cand, oh1, oh2, mask, slotpos, prod, tot = (
                g_sb(n, [P, NB, X]) for n in ("lg", "lg2", "cand", "oh1", "oh2", "mask", "slotpos", "prod", "tot"))
            m1, m2, i1, i2, dl, ex = (g_sb(n, [P, NB]) for n in ("m1", "m2", "i1", "i2", "dl", "ex"))
            gw = g_sb("gw", [P, 2, NB])
            SHB = 16
            scan = [g_sb(f"scan{k}", [P, SHB + NB, X]) for k in range(2)]
            SHX = 4
            cmp = g_sb("cmp", [P, X, TPE])
            tl = g_sb("tl", [P, X])
            scx = [g_sb(f"scx{k}", [P, SHX + X]) for k in range(2)]
            pos = g_sb("pos", [P, 2, NB])
            pos_i, hi_i, lo_i = (g_sb(n, [P, 2, NB], i32) for n in ("pos_i", "hi_i", "lo_i"))
            hi_f, lo_f = (g_sb(n, [P, 2, NB]) for n in ("hi_f", "lo_f"))
            oh_lo = g_sb("oh_lo", [P, 2, 128])
            oh_hi = g_sb("oh_hi", [P, 2, 2 * NH])
            padz = g_sb("padz", [128, NH])

        parts.append(weight_parts(1, ctx))
        hf = sb("hf", [128, KH, T])
        h_hi = sb("h_hi", [128, KH, T], f32r)
        h_lo = sb("h_lo", [128, KH, T], f32r)
        yg = sb("yg", [128, TH, D])
        y_hi = sb("y_hi", [128, KD, T], f32r)
        y_lo = sb("y_lo", [128, KD, T], f32r)
        otmp = sb("otmp", [128, TH, D])
        ost = sb("ost", [128, TH, D])
        gat_i = sb("gat_i", [128, TH], i32)
        add_i = sb("add_i", [128, TH], i32)

        with ExitStack() as gnn_ps:
            ps_agg = pb("ps_agg", [128, 2, KD, 512], gnn_ps)
            ps_lin = pb("ps_lin", [128, LIN, 512], gnn_ps)
            ps_m = pb("ps_m", [128, 512], gnn_ps)
        ps_h = pb("ps_h", [128, KH, T], ctx)
        ps_o = pb("ps_o", [128, TH, 512], ctx)
        ps_y = pb("ps_y", [128, KD, T], ctx)
        ps_edge = ps_lin[:, :, :].rearrange("p a d -> p (a d)")
        ps_yt = ps_agg[:, :, :, :].rearrange("p s k c -> p (s k) c")
        ps_b1 = ps_m[:, 256:256 + X * KH]
        ps_gate = ps_m[0:P, 0:NB * X]
        ps_rank = ps_edge[0:P, 0:NB * X].rearrange("p (b e) -> p b e", e=X)
        ps_tot = ps_edge[0:P, 512:512 + NB * X].rearrange("p (b e) -> p b e", e=X)
        ps_inv = ps_m[:, 0:2 * NH]

        s_const, s_edge_zero, s_xn_rows = sem("s_const"), sem("s_edge_zero"), sem("s_xn_rows")
        s_edges, s_small, s_b1 = sem("s_edges"), sem("s_small"), sem("s_b1")
        s_x = [sem(f"s_x{c}") for c in range(NC)]
        s_dve, s_pool = sem("s_dve"), sem("s_pool")
        s_var, s_sqrt, s_scale, s_xn = sem("s_var"), sem("s_sqrt"), sem("s_scale"), sem("s_xn")
        s_rows, s_cols, s_tables = sem("s_rows"), sem("s_cols"), sem("s_tables")
        s_b1_cols, s_b1_t = sem("s_b1_cols"), sem("s_b1_t")
        s_idx, s_window, s_agg, s_acc, s_next = sem("s_idx"), sem("s_window"), sem("s_agg"), sem("s_acc"), sem("s_next")
        s_xb = sem("s_xb")
        s_gathered = [sem(f"s_gathered{k}") for k in range(RING)]
        s_lin, s_sum = sem("s_lin"), sem("s_sum")
        s_y, s_yt, s_yt_sb, s_gate = sem("s_y"), sem("s_yt"), sem("s_yt_sb"), sem("s_gate")
        s_y_rows, s_out_rows, s_zero_rows = sem("s_y_rows"), sem("s_out_rows"), sem("s_zero_rows")
        s_delta, s_exp, s_mask, s_rank = sem("s_delta"), sem("s_exp"), sem("s_mask"), sem("s_rank")
        s_onehot, s_onehot_used, s_slots, s_route = sem("s_onehot"), sem("s_onehot_used"), sem("s_slots"), sem("s_route")
        s_raw, s_hi0, s_split0, s_hi, s_split = sem("s_raw"), sem("s_hi0"), sem("s_split0"), sem("s_hi"), sem("s_split")
        s_tile_in = [sem(f"s_tile_in{h}") for h in range(TH)]
        s_tile_t, s_y_hi, s_y_split = sem("s_tile_t"), sem("s_y_hi"), sem("s_y_split")
        s_hidden, s_gelu, s_h_hi, s_h_split = sem("s_hidden"), sem("s_gelu"), sem("s_h_hi"), sem("s_h_split")
        s_result, s_biased, s_staged, s_stage_free = sem("s_result"), sem("s_biased"), sem("s_staged"), sem("s_stage_free")
        s_index, s_go = sem("s_index"), sem("s_go")
        s_added = [sem(f"s_added{h}") for h in range(TH)]

        block = ctx.enter_context(nc.Block())

        def split_steps(e):
            w1_hi, w1_lo, w2_hi, w2_lo = parts[e % 2]
            for raw, hi, lo in ((w1_raw, w1_hi, w1_lo), (w2_raw, w2_hi, w2_lo)):
                raw, hi, lo = (flat(a[:, :, :]) for a in (raw, hi, lo))
                for c in range(0, raw.shape[1], SC):
                    yield raw[:, c:c + SC], hi[:, c:c + SC], lo[:, c:c + SC]

        @block.sync
        def _(sp):
            for c in range(NC):
                cs = slice(c * CB, (c + 1) * CB)
                for a, z in ((0, PA), (PA, P)):
                    sp.dma_start(x_sb[a:z, cs, :], x_v[a:z, cs, :]).then_inc(s_x[c], 16)
            full = (NG - 1) * GE

            def edge_rows(to, a):
                sp.dma_start(to[0:NG - 1, :], a[0:full].rearrange("(g j) -> g j", j=GE)).then_inc(s_edges, 16)
                sp.dma_start(to[NG - 1:NG, 0:LAST], a[full:E].rearrange("(g j) -> g j", g=1)).then_inc(s_edges, 16)

            for k, a in enumerate((dst, src)):
                edge_rows(e_int[:, k, :], a)
                sp.dma_start(e_int[NG - 1:NG, k, LAST:GE],
                             a[E - (GE - LAST):E].rearrange("(g j) -> g j", g=1)).then_inc(s_edges, 16)
            sp.wait_ge(s_edge_zero, 1)
            edge_rows(e_f[:, 2, :], edge_w)
            sp.dma_start(bias_bc[:, :], b_gnn.partition_broadcast(128)).then_inc(s_small, 16)
            sp.dma_start(bg_bc[:, :], b_gate.partition_broadcast(128)).then_inc(s_small, 16)
            sp.dma_start(wn_sb[:, :, :], w_gnn.rearrange("(k p) n -> p k n", p=128)).then_inc(s_small, 16)
            sp.dma_start(wg_sb[:, :, :], w_gate.rearrange("(k p) n -> p k n", p=128)).then_inc(s_small, 16)
            sp.dma_start(b2_bc[:, :, :], b2.partition_broadcast(128)).then_inc(s_small, 16)
            sp.dma_start(b1_in[:, :], b1.rearrange("e (c p) -> (e c) p", p=128)).then_inc(s_b1, 16)
            for c in range(NC):
                cs = slice(c * CB, (c + 1) * CB)
                sp.wait_ge(s_xn, (c + 1) * CB)
                for a, z in ((0, PA), (PA, P)):
                    sp.dma_start(xn_v[a:z, cs, :], y_sb[a:z, cs, :]).then_inc(s_xn_rows, 16)
            sp.wait_ge(s_const, 1)
            sp.dma_start(out[N:N + PAD_ROWS, :].rearrange("(a p) d -> p a d", p=128), zeros[:, :, :]).then_inc(s_zero_rows, 16)

            def load_weights(e):
                if e == 1:
                    sp.wait_ge(s_split0, SPLITS)
                if e > 1:
                    sp.wait_ge(s_split, SPLITS * (e - 1))
                sp.dma_start(w1_raw[:, :, :], w1[e].rearrange("(k p) h -> p k h", p=128)).then_inc(s_raw, 16)
                sp.dma_start(w2_raw[:, :, :], w2[e].rearrange("(k p) d -> p k d", p=128)).then_inc(s_raw, 16)

            load_weights(0)
            for c in range(NC):
                cs = slice(c * CB, (c + 1) * CB)
                sp.wait_ge(s_y, (c + 1) * CB)
                for a, z in ((0, PA), (PA, P)):
                    sp.dma_start(y_v[a:z, cs, :], y_sb[a:z, cs, :]).then_inc(s_y_rows, 16)
                    sp.dma_start(out_v[a:z, cs, :], x_sb[a:z, cs, :]).then_inc(s_out_rows, 16)
            for e in range(1, X):
                load_weights(e)
            sp.wait_ge(s_zero_rows, 16)
            sp.wait_ge(s_y_rows, 32 * NC)
            sp.wait_ge(s_out_rows, 32 * NC)

        @block.gpsimd
        def _(pool):
            own = Chain(pool, s_pool)

            def ramp(out_ap, pattern, base=0, step=0):
                own(pool.iota(out_ap, pattern, base=base, channel_multiplier=step, allow_small_or_imprecise_dtypes=True))

            pool.memset(e_f[:, 2, :], 0.0).then_inc(s_edge_zero, 1)
            ramp(iota_w[:, :], [[1, 128]])
            ramp(iota_x[:, :], [[1, X]])
            ramp(iota_mx[:, :], [[1, X]], base=-X)
            ramp(thr[:, :, :], [[0, X], [T, TPE]])
            ramp(thr_w[:, :], [[WIN, NWIN]])
            ramp(pad_row[:, :], [[0, NT], [128, TH]], base=N + 1, step=1)
            ramp(node1[:, :], [[1, NB]], base=1, step=NB)
            own(pool.memset(ones[:, :], 1.0))
            own(pool.memset(ident[:, :], 0.0))
            own(pool.affine_select(out=ident[:, :], in_=ident[:, :], compare_op=ALU.not_equal, fill=1.0,
                                   base=0, pattern=[[-1, 128]], channel_multiplier=1))
            own(pool.affine_select(out=tri[:, :], in_=ones[:, :], compare_op=ALU.is_gt, fill=0.0,
                                   base=0, pattern=[[1, 128]], channel_multiplier=-1))
            own(pool.memset(zeros[:, :, :], 0.0))
            own(pool.memset(slot_read[:, :], 0))
            own(pool.memset(slot_add[:, :], 0))
            own(pool.memset(slot_w[:, :], 0.0))
            own(pool.memset(x_sb[:, NB:NIT, :], 0.0))
            own(pool.memset(scan[0][:, 0:SHB, :], 0.0))
            own(pool.memset(scan[1][:, 0:SHB, :], 0.0))
            own(pool.memset(scx[0][:, 0:SHX], 0.0))
            own(pool.memset(scx[1][:, 0:SHX], 0.0))
            own(pool.memset(acc[:, :, :], 0.0))
            pool.sem_inc(s_const, 1)

            pool.wait_ge(s_tables, 1)
            n_pass = pool.value_load(passes[0:1, 0:1], min_val=1, max_val=NWIN)
            pool.wait_ge(s_xn_rows, 32 * NC)
            with pool.Fori(0, n_pass) as ps:
                with pool.Fori(0, NIT) as i:
                    for h in range(2):
                        pool.wait_ge(s_idx, (ps * NIT + i) * 2 + h + 1)
                        pool.sem_inc(s_go, 1)
                        for k in range(h * HALF, (h + 1) * HALF):
                            pool.indirect_dma_start(G[:, k, :], None, xn_d,
                                                    bass.IndirectOffsetOnAxis(idx_ring[:, k:k + 1], 0)).then_inc(s_gathered[k], 16)

            pool.wait_ge(s_raw, 32)
            for n, (raw, hi, lo) in enumerate(split_steps(0)):
                pool.tensor_copy(hi, raw).then_inc(s_hi0, 1)
                pool.wait_ge(s_hi0, n + 1)
                pool.tensor_tensor(lo, raw, hi.bitcast(f32), ALU.subtract).then_inc(s_split0, 1)

            pool.wait_ge(s_route, 1)
            pool.wait_ge(s_y_rows, 32 * NC)
            pool.wait_ge(s_out_rows, 32 * NC)
            pool.wait_ge(s_zero_rows, 16)

            def gather(tile, n):
                pool.tensor_copy(gat_i[:, :], slot_read[:, bass.ds(tile * TH, TH)]).then_inc(s_index, 1)
                pool.wait_ge(s_index, n)
                pool.sem_inc(s_go, 1)
                for h in range(TH):
                    pool.indirect_dma_start(yg[:, h, :], None, y_d,
                                            bass.IndirectOffsetOnAxis(gat_i[:, h:h + 1], 0)).then_inc(s_tile_in[h], 16)

            gather(0, 1)
            pool.wait_ge(s_tile_t, 1)
            gather(1, 2)
            pool.sem_inc(s_stage_free, 1)
            for e in range(X):
                first = pool.value_load(starts[0:1, e:e + 1], min_val=e, max_val=NT - 1)
                end = pool.value_load(starts[0:1, e + 1:e + 2], min_val=e + 1, max_val=NT)
                with pool.Fori(first, end) as g:
                    pool.wait_ge(s_tile_t, g + 2)
                    gather(g + 2, g * 2 + 3)
                    pool.tensor_copy(add_i[:, :], slot_add[:, bass.ds(g * TH, TH)]).then_inc(s_index, 1)
                    pool.wait_ge(s_index, g * 2 + 4)
                    pool.wait_ge(s_staged, (g + 1) * TH)
                    pool.sem_inc(s_go, 1)
                    for h in range(TH):
                        pool.indirect_dma_start(out, bass.IndirectOffsetOnAxis(add_i[:, h:h + 1], 0),
                                                ost[:, h, :], None, compute_op=ALU.add).then_inc(s_added[h], 16)
                    for h in range(TH):
                        pool.wait_ge(s_added[h], (g + 1) * 16)
                    pool.sem_inc(s_stage_free, 1)
            for h in range(TH):
                pool.wait_ge(s_tile_in[h], (end + 2) * 16)

        @block.scalar
        def _(act):
            def root(c, waited):
                cs = slice(c * CB, (c + 1) * CB)
                act.wait_ge(s_var, waited)
                nc.scalar.activation(sq[:, cs], ve[:, cs], ACT.Sqrt).then_inc(s_sqrt, 1)

            def normalise(c, waited, done):
                act.wait_ge(s_scale, waited)
                for b in range(c * CB, (c + 1) * CB):
                    nc.scalar.activation(y_sb[:, b, :], x_sb[:, b, :], ACT.Identity, bias=nmr[:, b:b + 1],
                                         scale=rstd[:, b:b + 1]).then_inc(done, 1)

            for c in range(NC + 1):
                if c < NC:
                    root(c, c + 1)
                if c >= 1:
                    normalise(c - 1, c, s_xn)

            act.wait_ge(s_tables, 2)
            n_pass = act.value_load(passes[0:1, 0:1], min_val=1, max_val=NWIN)
            src_v = flat(src_t[:, :, :])
            with act.Fori(0, n_pass) as ps:
                with act.Fori(0, NIT) as i:
                    for h in range(2):
                        act.wait_ge(s_agg, (ps * NIT + i) * BODY + (h + 1) * (BODY // 2))
                        nc.scalar.activation(idx_ring[:, h * HALF:(h + 1) * HALF],
                                             src_v[:, bass.ds(i * RING + h * HALF, HALF)], ACT.Copy).then_inc(s_idx, 1)

            for c in range(NC + 1):
                if c < NC:
                    root(c, NC + c + 1)
                if c >= 1:
                    normalise(c - 1, NC + c, s_y)
            act.wait_ge(s_delta, 1)
            nc.scalar.activation(ex[:, :], dl[:, :], ACT.Exp).then_inc(s_exp, 1)

            act.wait_ge(s_route, 1)
            act.wait_ge(s_b1_t, 1)
            for e in range(X):
                first = act.value_load(starts[0:1, e:e + 1], min_val=e, max_val=NT - 1)
                end = act.value_load(starts[0:1, e + 1:e + 2], min_val=e + 1, max_val=NT)
                if e + 1 < X:
                    act.wait_ge(s_raw, 32 * (e + 2))
                    if e >= 1:
                        act.wait_ge(s_result, first)
                    for raw, hi, lo in split_steps(e + 1):
                        nc.scalar.activation(hi, raw, ACT.Copy).then_inc(s_hi, 1)
                with act.Fori(first, end) as g:
                    for q in range(NQ):
                        act.wait_ge(s_hidden, g * NQ + q + 1)
                        for c in (2 * q, 2 * q + 1):
                            nc.scalar.activation(hf[:, c, :], ps_h[:, c, :], ACT.Gelu,
                                                 bias=b1_t[:, e * KH + c:e * KH + c + 1]).then_inc(s_gelu, 1)

        @block.tensor
        def _(pe):
            pe.wait_ge(s_const, 1)
            for k in range(3):
                if k < 2:
                    pe.wait_ge(s_rows, k + 1)
                else:
                    pe.wait_ge(s_edges, 16 * 8)
                for c in range(GT):
                    last = nc.tensor.transpose(ps_edge[:, k * 512 + c * NG:k * 512 + (c + 1) * NG],
                                               e_f[:, k, c * 128:(c + 1) * 128], ident[0:NG, 0:NG])
                last.then_inc(s_cols, 1)
            pe.wait_ge(s_rows, 3)
            for k in range(2):
                last = nc.tensor.transpose(ps_m[0:1, k * 128:k * 128 + NG], base_f[:, 2 * k:2 * k + 1],
                                           ident[0:NG, 0:NG])
            last.then_inc(s_cols, 1)
            pe.wait_ge(s_b1, 16)
            nc.tensor.transpose(ps_b1, b1_in[:, :], ident[0:X * KH, 0:X * KH]).then_inc(s_b1_cols, 1)

            pe.sem_inc(s_agg, BODY)
            pe.wait_ge(s_tables, 2)
            n_pass = pe.value_load(passes[0:1, 0:1], min_val=1, max_val=NWIN)
            with pe.Fori(0, n_pass) as ps:
                with pe.Fori(0, NIT) as i:
                    it = ps * NIT + i
                    for j in range(BODY):
                        pe.wait_ge(s_window, it * RING + (j + 1) * GT)
                        pe.wait_ge(s_acc, it * BODY + j + 1)
                        for c in range(GT):
                            k = j * GT + c
                            pe.wait_ge(s_gathered[k], it * 16 + 16)
                            for m in range(KD):
                                last = nc.tensor.matmul(ps_agg[:, j % 2, m, 0:WIN], G[:, k, m * 128:(m + 1) * 128],
                                                        S[:, k, :], start=(c == 0), stop=(c == GT - 1))
                        last.then_inc(s_agg, 1)

            pe.wait_ge(s_acc, n_pass * NG + 2)
            pe.wait_ge(s_small, 16 * 5)
            acc_v = acc[:, :, 0:N].rearrange("q k (p b) -> q k b p", b=NB)

            def linear(b):
                if b >= LIN:
                    pe.wait_ge(s_sum, b - LIN + 1)
                for m in range(KD):
                    last = nc.tensor.matmul(ps_lin[0:P, b % LIN, 0:D], acc_v[:, m, b, :], wn_sb[:, m, :],
                                            start=(m == 0), stop=(m == KD - 1))
                last.then_inc(s_lin, 1)

            def turn(b):
                pe.wait_ge(s_y, b + 1)
                if b >= 4:
                    pe.wait_ge(s_yt_sb, b - 3)
                for m in range(KD):
                    last = nc.tensor.transpose(ps_yt[:, b % 4, m * 128:m * 128 + P],
                                               y_sb[:, b, m * 128:(m + 1) * 128], ident[0:P, 0:P])
                last.then_inc(s_yt, 1)

            def gate(b):
                pe.wait_ge(s_yt_sb, b + 1)
                for m in range(KD):
                    last = nc.tensor.matmul(ps_gate[:, b * X:(b + 1) * X], yt_sb[:, b % CB, m, :], wg_sb[:, m, :],
                                            start=(m == 0), stop=(m == KD - 1))
                last.then_inc(s_gate, 1)

            for c in range(NC + 2):
                if c < NC:
                    for b in range(c * CB, (c + 1) * CB):
                        linear(b)
                if c >= 2:
                    for b in range((c - 2) * CB, (c - 1) * CB):
                        turn(b)
                        if b >= 1:
                            gate(b - 1)
            gate(NB - 1)

            pe.wait_ge(s_mask, 1)
            mk = flat(mask[:, :, :])
            nc.tensor.matmul(ps_edge[0:P, 0:NB * X], tri[0:P, 0:P], mk, start=True, stop=True)
            nc.tensor.matmul(ps_edge[0:P, 512:512 + NB * X], ones[0:P, 0:P], mk, start=True, stop=True).then_inc(s_rank, 1)
            zl, zr = zeros[0:P, 0, 0:128], zeros[0:P, 1, 0:2 * NH]
            nc.tensor.matmul(ps_inv, zl, zr, start=True, stop=False)
            with pe.Fori(0, NB) as b:
                for k in range(2):
                    pe.wait_ge(s_onehot, (b * 2 + k + 1) * 3)
                    nc.tensor.matmul(ps_inv, oh_lo[:, k, :], oh_hi[:, k, :], start=False, stop=False).then_inc(s_onehot_used, 1)
            nc.tensor.matmul(ps_inv, zl, zr, start=False, stop=True).then_inc(s_slots, 1)

            def transpose_tile(n):
                for h in range(TH):
                    pe.wait_ge(s_tile_in[h], n * 16)
                    for m in range(KD):
                        last = nc.tensor.transpose(ps_y[:, m, h * 128:(h + 1) * 128],
                                                   yg[:, h, m * 128:(m + 1) * 128], ident[:, :])
                last.then_inc(s_tile_t, 1)

            pe.wait_ge(s_route, 1)
            transpose_tile(1)
            pe.sem_inc(s_biased, 1)
            for e in range(X):
                w1_hi, w1_lo, w2_hi, w2_lo = parts[e % 2]
                first = pe.value_load(starts[0:1, e:e + 1], min_val=e, max_val=NT - 1)
                end = pe.value_load(starts[0:1, e + 1:e + 2], min_val=e + 1, max_val=NT)
                if e == 0:
                    pe.wait_ge(s_split0, SPLITS)
                else:
                    pe.wait_ge(s_split, SPLITS * e)
                with pe.Fori(first, end) as g:
                    pe.wait_ge(s_y_split, g + 1)
                    for q in range(NQ):
                        for c in (2 * q, 2 * q + 1):
                            terms = [(m, a, b) for m in range(KD) for a, b in
                                     ((w1_hi, y_hi), (w1_hi, y_lo), (w1_lo, y_hi))]
                            for n, (m, a, b) in enumerate(terms):
                                last = nc.tensor.matmul(ps_h[:, c, :], a[:, m, c * 128:(c + 1) * 128], b[:, m, :],
                                                        start=(n == 0), stop=(n == len(terms) - 1))
                        last.then_inc(s_hidden, 1)
                    transpose_tile(g + 2)
                    pe.wait_ge(s_biased, g + 1)
                    for q in range(NQ):
                        pe.wait_ge(s_h_split, g * NQ + q + 1)
                        for c in (2 * q, 2 * q + 1):
                            for n, (a, b) in enumerate(((h_hi, w2_hi), (h_hi, w2_lo), (h_lo, w2_hi))):
                                for h in range(TH):
                                    last = nc.tensor.matmul(ps_o[:, h, 0:D], a[:, c, h * 128:(h + 1) * 128], b[:, c, :],
                                                            start=(c == 0 and n == 0), stop=(c == KH - 1 and n == 2))
                    last.then_inc(s_result, 1)

        @block.vector
        def _(dve):
            own = Chain(dve, s_dve)
            V = nc.vector

            def stats(c, get):
                cs = slice(c * CB, (c + 1) * CB)
                for b in range(c * CB, (c + 1) * CB):
                    get(b)
                    own(V.bn_stats(bn[:, b, :], x_sb[:, b, :]))
                    own(V.bn_aggr(mv[:, b, :], bn[:, b, :]))
                V.tensor_scalar(ve[:, cs], mv[:, cs, 1], EPS, None, ALU.add).then_inc(s_var, 1)

            def scales(c, waited):
                cs = slice(c * CB, (c + 1) * CB)
                dve.wait_ge(s_sqrt, waited)
                own(V.reciprocal(nwt[:, cs], sq[:, cs]))
                own(V.tensor_tensor(nwt[:, cs], nwt[:, cs], ve[:, cs], ALU.mult))
                own(V.tensor_tensor(nwt[:, cs], nwt[:, cs], sq[:, cs], ALU.add))
                own(V.tensor_scalar(nwt[:, cs], nwt[:, cs], 0.5, None, ALU.mult))
                own(V.reciprocal(rstd[:, cs], nwt[:, cs]))
                V.scalar_tensor_tensor(out=nmr[:, cs], in0=mv[:, cs, 0], scalar=-1.0, in1=rstd[:, cs],
                                       op0=ALU.mult, op1=ALU.mult).then_inc(s_scale, 1)

            for c in range(NC + 1):
                if c < NC:
                    dve.wait_ge(s_x[c], 32)
                    stats(c, lambda b: None)
                if c >= 1:
                    scales(c - 1, c)

            dve.wait_ge(s_edges, 16 * 8)
            V.tensor_copy(e_f[:, 1, :], e_int[:, 1, :])
            own(V.tensor_copy(e_f[:, 0, :], e_int[:, 0, :]))
            own(V.tensor_reduce(base_f[:, 0:1], e_f[:, 0, :], AX.X, ALU.min))
            V.tensor_reduce(base_f[:, 1:2], e_f[:, 0, :], AX.X, ALU.max)
            own(V.tensor_scalar(e_f[:, 0, :], e_f[:, 0, :], base_f[:, 0:1], None, ALU.subtract))
            own(V.tensor_tensor(base_f[:, 2:3], base_f[:, 1:2], base_f[:, 0:1], ALU.subtract))
            dve.sem_inc(s_rows, 3)
            dve.wait_ge(s_const, 1)
            for k, (to, shape_i) in enumerate(((rel_t, 0), (src_t, 1), (ew_t, 2))):
                dve.wait_ge(s_cols, k + 1)
                own(V.tensor_copy(to[:, :, :], ps_edge[:, k * 512:k * 512 + GT * NG].rearrange("p (c g) -> p g c", g=NG)))
            dve.wait_ge(s_cols, 4)
            dve.wait_ge(s_b1_cols, 1)
            own(V.tensor_copy(base_r[:, :], ps_m[0:1, 0:NG]))
            own(V.tensor_copy(base_i[:, :], base_r[:, :]))
            own(V.tensor_reduce(span[:, 0:1], ps_m[0:1, 128:128 + NG], AX.X, ALU.max))
            own(V.tensor_scalar(span[:, 2:2 + NWIN], thr_w[:, :], span[:, 0:1], None, ALU.is_le))
            own(V.tensor_reduce(span[:, 1:2], span[:, 2:2 + NWIN], AX.X, ALU.add))
            own(V.tensor_copy(passes[:, :], span[:, 1:2]))
            dve.sem_inc(s_tables, 2)
            V.tensor_copy(b1_t[:, :], ps_b1).then_inc(s_b1_t, 1)
            dve.wait_ge(s_xn_rows, 32 * NC)
            dve.wait_ge(s_small, 16 * 5)

            dve.sem_inc(s_acc, 2)
            n_pass = dve.value_load(passes[0:1, 0:1], min_val=1, max_val=NWIN)
            rel_v, ew_v = flat(rel_t[:, :, :]), flat(ew_t[:, :, :])
            with dve.Fori(0, n_pass) as ps:
                with dve.Fori(0, NIT) as i:
                    it = ps * NIT + i
                    for k in range(RING):
                        if k % HALF == 0:
                            dve.wait_ge(s_agg, it * BODY + (k // HALF + 1) * (BODY // 2))
                        t = bass.ds(i * RING + k, 1)
                        V.tensor_scalar(S[:, k, :], iota_w[:, 0:WIN], rel_v[:, t], ew_v[:, t],
                                        ALU.is_equal, ALU.mult).then_inc(s_window, 1)
                    bs = bass.ds(i, 1)
                    V.tensor_tensor(flat(y_sb[:, bs, :]), flat(x_sb[:, bs, :]), bias_bc[0:P, :], ALU.add).then_inc(s_xb, 1)
                    for j in range(BODY):
                        base = dve.value_load(base_i[0:1, bass.ds(i * BODY + j, 1)], min_val=0, max_val=N)
                        dve.wait_ge(s_agg, it * BODY + j + 1 + BODY)
                        dve.wait_ge(s_acc, it * BODY + j + 2)
                        V.tensor_tensor(acc[:, :, bass.ds(base, WIN)], acc[:, :, bass.ds(base, WIN)],
                                        ps_agg[:, j % 2, :, 0:WIN], ALU.add).then_inc(s_acc, 1)
                dve.wait_ge(s_window, (ps + 1) * (NIT * RING))
                V.tensor_scalar(rel_v, rel_v, float(-WIN), None, ALU.add).then_inc(s_next, 1)
                V.tensor_scalar(base_r[:, :], base_r[:, :], float(WIN), float(N), ALU.add, ALU.min).then_inc(s_next, 1)
                dve.wait_ge(s_next, ps * 3 + 2)
                V.tensor_copy(base_i[:, :], base_r[:, :]).then_inc(s_next, 1)
                dve.wait_ge(s_next, ps * 3 + 3)

            dve.wait_ge(s_xb, n_pass * NIT)

            def add_up(b):
                dve.wait_ge(s_lin, b + 1)
                V.tensor_tensor(x_sb[:, b, :], ps_lin[0:P, b % LIN, 0:D], y_sb[:, b, :], ALU.add).then_inc(s_sum, 1)
                dve.wait_ge(s_sum, b + 1)

            def logits(c):
                for b in range(c * CB, (c + 1) * CB):
                    dve.wait_ge(s_yt, b + 1)
                    if b >= CB:
                        dve.wait_ge(s_gate, b - CB + 1)
                    V.tensor_copy(yt_sb[:, b % CB, :, :],
                                  ps_yt[:, b % 4, 0:KD * 128].rearrange("q (k p) -> q k p", p=128)[:, :, 0:P]).then_inc(s_yt_sb, 1)

            for c in range(NC + 2):
                if c < NC:
                    stats(c, add_up)
                if 1 <= c <= NC:
                    scales(c - 1, NC + c)
                if c >= 2:
                    logits(c - 2)

            def bc(a, n=X):
                return a.unsqueeze(2).to_broadcast([P, NB, n])

            def bx(a):
                return a.unsqueeze(1).to_broadcast([P, NB, X])

            dve.wait_ge(s_gate, NB)
            own(V.tensor_tensor(lg[:, :, :], ps_gate.rearrange("p (b e) -> p b e", e=X), bx(bg_bc[0:P, :]), ALU.add))

            def choose(logit, m, i, oh):
                own(V.tensor_reduce(m[:, :], logit[:, :, :], AX.X, ALU.max))
                own(V.tensor_tensor(cand[:, :, :], logit[:, :, :], bc(m[:, :]), ALU.is_equal))
                own(V.scalar_tensor_tensor(out=cand[:, :, :], in0=cand[:, :, :], scalar=float(-X), in1=bx(iota_x[0:P, :]),
                                           op0=ALU.mult, op1=ALU.add))
                own(V.tensor_reduce(i[:, :], cand[:, :, :], AX.X, ALU.min))
                own(V.tensor_tensor(oh[:, :, :], bx(iota_mx[0:P, :]), bc(i[:, :]), ALU.is_equal))

            choose(lg, m1, i1, oh1)
            own(V.scalar_tensor_tensor(out=lg2[:, :, :], in0=oh1[:, :, :], scalar=NEG, in1=lg[:, :, :],
                                       op0=ALU.mult, op1=ALU.add))
            choose(lg2, m2, i2, oh2)
            V.tensor_tensor(mask[:, :, :], oh1[:, :, :], oh2[:, :, :], ALU.add).then_inc(s_mask, 1)
            V.tensor_tensor(dl[:, :], m2[:, :], m1[:, :], ALU.subtract).then_inc(s_delta, 1)
            dve.wait_ge(s_exp, 1)
            own(V.tensor_scalar(dl[:, :], ex[:, :], 1.0, None, ALU.add))
            own(V.reciprocal(gw[:, 0, :], dl[:, :]))
            own(V.tensor_tensor(gw[:, 1, :], ex[:, :], gw[:, 0, :], ALU.mult))

            dve.wait_ge(s_rank, 1)
            V.tensor_copy(tot[:, :, :], ps_tot)
            own(V.tensor_copy(scan[0][:, SHB:SHB + NB, :], ps_tot))
            cur, step = 0, 1
            while step < NB:
                a, b = scan[cur], scan[1 - cur]
                own(V.tensor_tensor(b[:, SHB:SHB + NB, :], a[:, SHB:SHB + NB, :], a[:, SHB - step:SHB + NB - step, :], ALU.add))
                cur, step = 1 - cur, step * 2
            run = scan[cur]
            chosen = run[:, SHB + NB - 1, :]
            own(V.tensor_tensor(cmp[:, :, :], thr[0:P, :, :], chosen.unsqueeze(2).to_broadcast([P, X, TPE]), ALU.is_lt))
            own(V.tensor_reduce(tl[:, :], cmp[:, :, :], AX.X, ALU.add))
            own(V.tensor_scalar(tl[:, :], tl[:, :], 1.0, None, ALU.max))
            own(V.tensor_copy(scx[0][:, SHX:SHX + X], tl[:, :]))
            cx, step = 0, 1
            while step < X:
                a, b = scx[cx], scx[1 - cx]
                own(V.tensor_tensor(b[:, SHX:SHX + X], a[:, SHX:SHX + X], a[:, SHX - step:SHX + X - step], ALU.add))
                cx, step = 1 - cx, step * 2
            before = scx[cx][:, SHX - 1:SHX + X - 1]
            own(V.tensor_copy(starts[:, :], scx[cx][0:1, SHX - 1:SHX + X]))
            own(V.tensor_tensor(slotpos[:, :, :], run[:, SHB:SHB + NB, :], tot[:, :, :], ALU.subtract))
            own(V.tensor_tensor(slotpos[:, :, :], slotpos[:, :, :], ps_rank, ALU.add))
            own(V.scalar_tensor_tensor(out=slotpos[:, :, :], in0=bx(before), scalar=float(T), in1=slotpos[:, :, :],
                                       op0=ALU.mult, op1=ALU.add))
            for k, oh in enumerate((oh1, oh2)):
                own(V.tensor_tensor(prod[:, :, :], oh[:, :, :], slotpos[:, :, :], ALU.mult))
                own(V.tensor_reduce(pos[:, k, :], prod[:, :, :], AX.X, ALU.add))
            own(V.tensor_copy(pos_i[:, :, :], pos[:, :, :]))
            own(V.tensor_scalar(hi_i[:, :, :], pos_i[:, :, :], 7, None, ALU.arith_shift_right))
            own(V.tensor_scalar(lo_i[:, :, :], pos_i[:, :, :], 127, None, ALU.bitwise_and))
            own(V.tensor_copy(hi_f[:, :, :], hi_i[:, :, :]))
            own(V.tensor_copy(lo_f[:, :, :], lo_i[:, :, :]))
            dve.sem_inc(s_onehot_used, 2)
            with dve.Fori(0, NB) as b:
                bs = bass.ds(b, 1)
                for k in range(2):
                    dve.wait_ge(s_onehot_used, b * 2 + k + 1)
                    V.tensor_scalar(oh_lo[:, k, :], iota_w[0:P, :], lo_f[:, k, bs], None, ALU.is_equal).then_inc(s_onehot, 1)
                    V.tensor_scalar(oh_hi[:, k, 0:NH], iota_w[0:P, 0:NH], hi_f[:, k, bs], node1[0:P, bs],
                                    ALU.is_equal, ALU.mult).then_inc(s_onehot, 1)
                    V.tensor_scalar(oh_hi[:, k, NH:2 * NH], iota_w[0:P, 0:NH], hi_f[:, k, bs], gw[:, k, bs],
                                    ALU.is_equal, ALU.mult).then_inc(s_onehot, 1)
            dve.wait_ge(s_slots, 1)
            own(V.tensor_copy(slot_w[:, 0:NH], ps_inv[:, NH:2 * NH]))
            own(V.tensor_scalar(slot_read[:, 0:NH], ps_inv[:, 0:NH], -1.0, 0.0, ALU.add, ALU.max))
            own(V.scalar_tensor_tensor(out=padz[:, :], in0=ps_inv[:, 0:NH], scalar=0.0, in1=pad_row[:, :],
                                       op0=ALU.is_equal, op1=ALU.mult))
            own(V.scalar_tensor_tensor(out=slot_add[:, 0:NH], in0=padz[:, :], scalar=-1.0, in1=ps_inv[:, 0:NH],
                                       op0=ALU.add, op1=ALU.add))
            dve.sem_inc(s_route, 1)

            def split_tile(n):
                dve.wait_ge(s_tile_t, n)
                V.tensor_copy(y_hi[:, :, :], ps_y[:, :, :]).then_inc(s_y_hi, 1)
                dve.wait_ge(s_y_hi, n)
                V.tensor_tensor(y_lo[:, :, :], ps_y[:, :, :], y_hi[:, :, :].bitcast(f32), ALU.subtract).then_inc(s_y_split, 1)

            split_tile(1)
            for e in range(X):
                first = dve.value_load(starts[0:1, e:e + 1], min_val=e, max_val=NT - 1)
                end = dve.value_load(starts[0:1, e + 1:e + 2], min_val=e + 1, max_val=NT)
                if e + 1 < X:
                    for n, (raw, hi, lo) in enumerate(split_steps(e + 1)):
                        dve.wait_ge(s_hi, SPLITS * e + n + 1)
                        V.tensor_tensor(lo, raw, hi.bitcast(f32), ALU.subtract).then_inc(s_split, 1)
                with dve.Fori(first, end) as g:
                    for q in range(NQ):
                        qs = slice(2 * q, 2 * q + 2)
                        dve.wait_ge(s_gelu, (g * NQ + q + 1) * 2)
                        V.tensor_copy(h_hi[:, qs, :], hf[:, qs, :]).then_inc(s_h_hi, 1)
                        dve.wait_ge(s_h_hi, g * NQ + q + 1)
                        V.tensor_tensor(h_lo[:, qs, :], hf[:, qs, :], h_hi[:, qs, :].bitcast(f32),
                                        ALU.subtract).then_inc(s_h_split, 1)
                    split_tile(g + 2)
                    dve.wait_ge(s_result, g + 1)
                    V.tensor_tensor(otmp[:, :, :], ps_o[:, :, 0:D], b2_bc[:, e, :].unsqueeze(1).to_broadcast([128, TH, D]),
                                    ALU.add).then_inc(s_biased, 1)
                    dve.wait_ge(s_biased, g + 2)
                    dve.wait_ge(s_stage_free, g + 1)
                    for h in range(TH):
                        V.tensor_scalar(ost[:, h, :], otmp[:, h, :], slot_w[:, bass.ds(g * TH + h, 1)], None,
                                        ALU.mult).then_inc(s_staged, 1)


_INS = ["x", "src", "dst", "edge_weight", "L0_gnn_weight", "L0_gnn_bias", "L0_ffn_Wg", "L0_ffn_bg",
        "L0_ffn_W1", "L0_ffn_b1", "L0_ffn_W2", "L0_ffn_b2"]


def kernel(**inputs):
    import numpy as np
    import concourse.bacc as bacc
    from concourse.bass_utils import run_bass_kernel_spmd

    nc = bacc.Bacc("TRN2", target_bir_lowering=False, num_devices=1)
    arrays, args = {}, []
    for name in _INS:
        a = np.ascontiguousarray(inputs[name])
        arrays[f"in_{name}"] = a
        args.append(nc.dram_tensor(f"in_{name}", a.shape, mybir.dt.from_np(a.dtype), kind="ExternalInput").ap())
    nodes, features = inputs["x"].shape
    args.append(nc.dram_tensor("result", (nodes + PAD_ROWS, features), mybir.dt.float32, kind="ExternalOutput").ap())
    gnn_moe_layer(nc, *args)
    run = run_bass_kernel_spmd(nc, [arrays], core_ids=[0])
    return run.results[0]["result"][:nodes]
```

```python
import concourse.bass as bass
from concourse import mybir
from contextlib import ExitStack

PAD_ROWS = 256
CHUNK_BLOCKS = ((5, 4, 3), (5, 5, 3))


class Order:

    def __init__(self, eng, sem):
        self.eng, self.sem, self.n = eng, sem, 0

    def mark(self, ins):
        self.n += 1
        ins.then_inc(self.sem, 1)
        return self.n

    def need(self, n):
        self.eng.wait_ge(self.sem, n)

    def own(self, ins):
        self.need(self.mark(ins))


class EdgeSems:

    def __init__(self, sem, name, ring):
        self.idx = sem(f"s_{name}_idx")
        self.window = sem(f"s_{name}_window")
        self.used = sem(f"s_{name}_used")
        self.acc = sem(f"s_{name}_acc")
        self.gathered = [sem(f"s_{name}_gathered{k}") for k in range(ring)]


class Chunk:

    def __init__(self, index, first_block, blocks, rows):
        self.index, self.first, self.blocks, self.nodes = index, first_block * rows, blocks, blocks * rows
        self.a, self.z = first_block, first_block + blocks


class NodeSet:

    def __init__(self, index, chunks, tile, experts):
        self.index, self.chunks = index, chunks
        self.first_block, self.blocks = chunks[0].a, chunks[-1].z - chunks[0].a
        self.nodes = sum(c.nodes for c in chunks)
        self.max_tiles = (2 * self.nodes - experts) // tile + experts


class ChunkSems:

    def __init__(self, sem, chunks):
        self.x = [sem(f"s_chunk_x{c.index}") for c in chunks]
        self.stored = [sem(f"s_stored{c.index}") for c in chunks]
        self.lin, self.sum, self.var, self.root, self.scale = (
            sem(f"s_{n}") for n in ("lin", "sum", "chunk_var", "chunk_root", "chunk_scale"))
        self.y, self.yt, self.yt_sb, self.gate, self.logits = (
            sem(f"s_{n}") for n in ("y", "yt", "yt_sb", "gate", "logits"))


class SetSems:

    def __init__(self, sem, s, halves):
        def own(what):
            return sem(f"s{s.index}_{what}")

        self.delta, self.exp, self.mask, self.rank = map(own, ("delta", "exp", "mask", "rank"))
        self.onehot, self.onehot_used, self.route = map(own, ("onehot", "onehot_used", "route"))
        self.tile_in = [own(f"tile_in{h}") for h in range(halves)]
        self.tile_t, self.y_hi, self.y_split = map(own, ("tile_t", "y_hi", "y_split"))
        self.hidden, self.gelu, self.h_hi, self.h_split = map(own, ("hidden", "gelu", "h_hi", "h_split"))
        self.result, self.biased, self.staged, self.index = map(own, ("result", "biased", "staged", "index"))
        self.added = [own(f"added{h}") for h in range(halves)]


def gnn_moe_layer(nc, x, src, dst, edge_w, w_gnn, b_gnn, w_gate, b_gate, w1, b1, w2, b2, out):
    f32, f32r, i32 = mybir.dt.float32, mybir.dt.float32r, mybir.dt.int32
    ACT, ALU, AX = mybir.ActivationFunctionType, mybir.AluOpType, mybir.AxisListType

    N, D = x.shape
    E = src.shape[0]
    X = w_gate.shape[1]
    H = w1.shape[2]
    KD, KH = D // 128, H // 128
    EPS = 1e-5
    NEG = -3.0e38

    P, NB, CB = 125, 25, 5
    NC = NB // CB
    assert P * NB == N
    PA = 112

    T = 256
    TH = T // 128
    NQ = KH // 2
    SC = 1024
    STEPS = KD * H // SC
    assert PAD_ROWS == T and KD * H == KH * D

    GT, WIN = 4, 64
    GE = GT * 128
    NG = -(-E // GE)
    NP = NG // 2
    RING = 2 * GT
    assert NP * 2 == NG
    LAST = E - (NG - 1) * GE
    NWIN = -(-N // WIN)

    CHUNKS = []
    for n in CHUNK_BLOCKS[0] + CHUNK_BLOCKS[1]:
        CHUNKS.append(Chunk(len(CHUNKS), CHUNKS[-1].z if CHUNKS else 0, n, P))
    L0 = len(CHUNK_BLOCKS[0])
    SETS = [NodeSet(0, CHUNKS[:L0], T, X), NodeSet(1, CHUNKS[L0:], T, X)]
    BM = max(s.blocks for s in SETS)
    CM = max(c.blocks for c in CHUNKS)
    NH = TH * max(s.max_tiles for s in SETS)
    NHP = NH + 2 * TH
    TPE = -(-max(s.nodes for s in SETS) // T)
    assert CHUNKS[-1].z == NB
    RB = 3

    COMPLETE = [-(-((c.first + c.nodes) * E * 100 // N + 36 * 2 * GE) // (200 * GE)) for c in CHUNKS[:-1]] + [NP]
    DURING = 5
    U0 = COMPLETE[L0 - 1] + DURING
    UMAX = max(U0 + SETS[0].max_tiles, NP) + 1
    REST = 6
    assert NP - REST + 1 >= COMPLETE[-2]

    xn_d = nc.dram_tensor("xn_d", (N, D), f32, kind="Internal").ap()
    y_d = [nc.dram_tensor(f"y{s.index}_d", (s.nodes, D), f32, kind="Internal").ap() for s in SETS]

    def by_partition(a, blocks):
        return a.rearrange("(p b) d -> p b d", b=blocks)

    def of_chunk(a, c, first=0):
        return by_partition(a[c.first - first:c.first - first + c.nodes, :], c.blocks)

    def flat(a):
        return a.rearrange("p a b -> p (a b)")

    SPANS = ((0, PA), (PA, P))

    with ExitStack() as ctx:
        def sb(name, shape, dt=f32, stack=ctx):
            return stack.enter_context(nc.sbuf_tensor(name, shape, dt))

        def pb(name, shape):
            return ctx.enter_context(nc.psum_tensor(name, shape, f32))

        def sem(name):
            return ctx.enter_context(nc.semaphore(name))

        ident = sb("ident", [128, 128])
        iota_w = sb("iota_w", [128, 128])
        iota_x = sb("iota_x", [128, X])
        iota_mx = sb("iota_mx", [128, X])
        tri = sb("tri", [128, 128])
        ones = sb("ones", [128, 128])
        zeros = sb("zeros", [128, PAD_ROWS // 128, D])
        thr = sb("thr", [128, X, TPE])
        thr_w = sb("thr_w", [1, NWIN])
        pad_i = sb("pad_i", [128, TH], i32)
        pad_row = [sb(f"pad_row{s.index}", [128, NH]) for s in SETS]
        node1 = [sb(f"node1_{s.index}", [128, s.blocks]) for s in SETS]
        chunk_end = sb("chunk_end", [1, len(CHUNKS) - 1])
        bias_bc = sb("bias_bc", [128, D])
        bg_bc = sb("bg_bc", [128, X])
        wg_sb = sb("wg_sb", [128, KD, X])
        wn_sb = sb("wn_sb", [128, KD, D])
        b1_in = sb("b1_in", [X * KH, 128])
        b1_t = sb("b1_t", [128, X * KH])
        b2_bc = sb("b2_bc", [128, X, D])

        rel_t = sb("rel_t", [128, 2 * UMAX, GT])
        src_t = sb("src_t", [128, 2 * UMAX, GT], i32)
        ew_t = sb("ew_t", [128, 2 * UMAX, GT])
        base_r = sb("base_r", [1, 2 * UMAX])
        base_i = sb("base_i", [1, 2 * UMAX], i32)
        span = sb("span", [1, NWIN + 4])
        least = sb("least", [1, 2, len(CHUNKS) - 1])
        cuts = sb("cuts", [1, 3, REST + 1])
        cuts_i = sb("cuts_i", [1, 2, REST + 1], i32)
        cut_lo = sb("cut_lo", [1, REST + 1])
        before_i = sb("before_i", [1, 1], i32)
        acc = sb("acc", [128, KD, N + WIN])
        idx_ring = sb("idx_ring", [128, RING], i32)
        G = sb("G", [128, RING, D])
        S = sb("S", [128, RING, WIN])

        xr = sb("xr", [P, 2, CM, D])
        yr = sb("yr", [P, 2, CM, D])
        yt_sb = sb("yt_sb", [128, 2, KD, P])
        bn = sb("bn", [P, NB, 6])
        mv = sb("mv", [P, NB, 2])
        ve, sq, nwt, rstd, nmr = (sb(n, [P, NB]) for n in ("ve", "sq", "nwt", "rstd", "nmr"))
        lg, lg2, cand, oh1, oh2, mask, slotpos, prod, tot = (
            sb(n, [P, BM, X]) for n in ("lg", "lg2", "cand", "oh1", "oh2", "mask", "slotpos", "prod", "tot"))
        m1, m2, i1, i2, dl, ex = (sb(n, [P, BM]) for n in ("m1", "m2", "i1", "i2", "dl", "ex"))
        gw = sb("gw", [P, 2, BM])
        SHB, SHX = 8, 4
        scan = [sb(f"scan{k}", [P, SHB + BM, X]) for k in range(2)]
        cmp = sb("cmp", [P, X, TPE])
        tl = sb("tl", [P, X])
        scx = [sb(f"scx{k}", [P, SHX + X]) for k in range(2)]
        pos = sb("pos", [P, 2, BM])
        pos_i, hi_i, lo_i = (sb(n, [P, 2, BM], i32) for n in ("pos_i", "hi_i", "lo_i"))
        hi_f, lo_f = (sb(n, [P, 2, BM]) for n in ("hi_f", "lo_f"))
        padz = sb("padz", [128, NH])
        slot_read = [sb(f"slot_read{s.index}", [128, NHP], i32) for s in SETS]
        slot_add = [sb(f"slot_add{s.index}", [128, NHP], i32) for s in SETS]
        slot_w = [sb(f"slot_w{s.index}", [128, NHP]) for s in SETS]
        starts = [sb(f"starts{s.index}", [1, X + 1], i32) for s in SETS]

        w1_raw = sb("w1_raw", [128, KD, H])
        w2_raw = sb("w2_raw", [128, KH, D])

        def weight_parts(k):
            return [sb(f"{n}_{k}", shape, f32r) for n, shape in
                    (("w1_hi", [128, KD, H]), ("w1_lo", [128, KD, H]), ("w2_hi", [128, KH, D]), ("w2_lo", [128, KH, D]))]

        parts = [weight_parts(0)]
        with ExitStack() as early:
            x_sb = sb("x_sb", [P, NB, D], f32, early)
            xn_sb = sb("xn_sb", [P, NB, D], f32, early)
            e_int, xe_int = (sb(n, [NG, GE], i32, early) for n in ("e_int", "xe_int"))
            e_f, xe_f, we_f = (sb(n, [NG, GE], f32, early) for n in ("e_f", "xe_f", "we_f"))
            base_f = sb("base_f", [NG, 3], f32, early)
        parts.append(weight_parts(1))
        with ExitStack() as routing:
            oh_lo = sb("oh_lo", [P, 2, 2, RB, 128], f32, routing)
            oh_hi = sb("oh_hi", [P, 2, 2, RB, 2, NH], f32, routing)
        hf = sb("hf", [128, 2, 2, T])
        h_hi = sb("h_hi", [128, KH, T], f32r)
        h_lo = sb("h_lo", [128, KH, T], f32r)
        yg = sb("yg", [128, TH, D])
        y_hi = sb("y_hi", [128, KD, T], f32r)
        y_lo = sb("y_lo", [128, KD, T], f32r)
        ost = sb("ost", [128, TH, D])
        gat_i = sb("gat_i", [128, TH], i32)
        add_i = sb("add_i", [128, TH], i32)

        ps_h = pb("ps_h", [128, 2, 512])
        ps_o = pb("ps_o", [128, 2, 512])
        ps_y = pb("ps_y", [128, 512])
        ps_m = pb("ps_m", [128, 512])
        ps_agg = pb("ps_agg", [128, 2, 512])
        ps_b1 = ps_m[:, 256:256 + X * KH]
        places = (ps_m, ps_y)
        ps_gate = ps_o[0:P, 0, :]

        s_const, s_edge_zero, s_xn_rows, s_xn = sem("s_const"), sem("s_edge_zero"), sem("s_xn_rows"), sem("s_xn")
        s_dst, s_src, s_weights, s_small, s_b1 = sem("s_dst"), sem("s_src"), sem("s_weights"), sem("s_small"), sem("s_b1")
        s_x = [sem(f"s_x{c}") for c in range(NC)]
        s_dve, s_pool, s_zero_rows, s_go = sem("s_dve"), sem("s_pool"), sem("s_zero_rows"), sem("s_go")
        s_over, s_cuts = sem("s_over"), sem("s_cuts")
        s_var, s_root, s_scale = sem("s_var"), sem("s_root"), sem("s_scale")
        s_rows, s_cols, s_tables, s_b1_t, s_next = sem("s_rows"), sem("s_cols"), sem("s_tables"), sem("s_b1_t"), sem("s_next")
        s_raw1, s_raw2, s_hi1, s_hi2, s_split1, s_split2 = (
            sem(f"s_{n}") for n in ("raw1", "raw2", "hi1", "hi2", "split1", "split2"))
        pre, main = EdgeSems(sem, "pre", RING), EdgeSems(sem, "main", RING)
        ch = ChunkSems(sem, CHUNKS)
        sems = [SetSems(sem, s, TH) for s in SETS]

        block = ctx.enter_context(nc.Block())

        def split_steps(x, which):
            w1_hi, w1_lo, w2_hi, w2_lo = parts[x % 2]
            raw, hi, lo = (w1_raw, w1_hi, w1_lo) if which == 1 else (w2_raw, w2_hi, w2_lo)
            raw, hi, lo = (flat(a[:, :, :]) for a in (raw, hi, lo))
            return [(raw[:, c:c + SC], hi[:, c:c + SC], lo[:, c:c + SC]) for c in range(0, KD * H, SC)]

        BESIDE = {name: COMPLETE[L0 - 1] + 2 + n for n, name in enumerate(("chosen", "ranked", "half"))}
        assert DURING == 2 + len(BESIDE)

        def steps_of(blocks):
            return [(b, min(b + RB, blocks)) for b in range(0, blocks, RB)]

        def cut_of(eng, i):
            a = eng.value_load(cuts_i[0:1, 0, i:i + 1], min_val=0, max_val=UMAX - 1)
            z = eng.value_load(cuts_i[0:1, 0, i + 1:i + 2], min_val=0, max_val=UMAX - 1)
            return a, z, eng.value_load(cuts_i[0:1, 1, i:i + 1], min_val=0, max_val=UMAX - 1)

        @block.sync
        def _(sp):
            x_v, xn_v = by_partition(x, NB), by_partition(xn_d, NB)
            for c in range(NC):
                cs = slice(c * CB, (c + 1) * CB)
                for a, z in SPANS:
                    sp.dma_start(x_sb[a:z, cs, :], x_v[a:z, cs, :]).then_inc(s_x[c], 16)
            full = (NG - 1) * GE

            def edge_rows(to, a, done, fill):
                sp.dma_start(to[0:NG - 1, :], a[0:full].rearrange("(g j) -> g j", j=GE)).then_inc(done, 16)
                sp.dma_start(to[NG - 1:NG, 0:LAST], a[full:E].rearrange("(g j) -> g j", g=1)).then_inc(done, 16)
                if fill:
                    sp.dma_start(to[NG - 1:NG, LAST:GE],
                                 a[E - (GE - LAST):E].rearrange("(g j) -> g j", g=1)).then_inc(done, 16)

            edge_rows(e_int, dst, s_dst, True)
            edge_rows(xe_int, src, s_src, True)
            sp.wait_ge(s_edge_zero, 1)
            edge_rows(we_f, edge_w, s_weights, False)
            sp.dma_start(b1_in[:, :], b1.rearrange("e (c p) -> (e c) p", p=128)).then_inc(s_b1, 16)
            for c in range(NC):
                cs = slice(c * CB, (c + 1) * CB)
                sp.wait_ge(s_xn, (c + 1) * CB)
                for a, z in SPANS:
                    sp.dma_start(xn_v[a:z, cs, :], xn_sb[a:z, cs, :]).then_inc(s_xn_rows, 16)
            sp.dma_start(bias_bc[:, :], b_gnn.partition_broadcast(128)).then_inc(s_small, 16)
            sp.dma_start(bg_bc[:, :], b_gate.partition_broadcast(128)).then_inc(s_small, 16)
            sp.dma_start(wn_sb[:, :, :], w_gnn.rearrange("(k p) n -> p k n", p=128)).then_inc(s_small, 16)
            sp.dma_start(wg_sb[:, :, :], w_gate.rearrange("(k p) n -> p k n", p=128)).then_inc(s_small, 16)
            sp.dma_start(b2_bc[:, :, :], b2.partition_broadcast(128)).then_inc(s_small, 16)
            sp.wait_ge(s_const, 1)
            sp.dma_start(out[N:N + PAD_ROWS, :].rearrange("(a p) d -> p a d", p=128), zeros[:, :, :]).then_inc(s_zero_rows, 16)

            def load_weights(x):
                if x:
                    sp.wait_ge(s_split1, STEPS * x)
                sp.dma_start(w1_raw[:, :, :], w1[x % X].rearrange("(k p) h -> p k h", p=128)).then_inc(s_raw1, 16)
                if x:
                    sp.wait_ge(s_split2, STEPS * x)
                sp.dma_start(w2_raw[:, :, :], w2[x % X].rearrange("(k p) d -> p k d", p=128)).then_inc(s_raw2, 16)

            def load_x(c):
                for a, z in SPANS:
                    sp.dma_start(xr[a:z, c.index % 2, 0:c.blocks, :], of_chunk(x, c)[a:z, :, :]).then_inc(ch.x[c.index], 16)

            load_weights(0)
            load_x(CHUNKS[0])
            load_x(CHUNKS[1])
            load_weights(1)
            for s in SETS:
                first = s.chunks[0].first
                for c in s.chunks:
                    sp.wait_ge(ch.y, c.z)
                    for a, z in SPANS:
                        rows = (slice(a, z), c.index % 2, slice(0, c.blocks), slice(None))
                        sp.dma_start(of_chunk(y_d[s.index], c, first)[a:z, :, :], yr[rows]).then_inc(ch.stored[c.index], 16)
                        sp.dma_start(of_chunk(out, c)[a:z, :, :], xr[rows]).then_inc(ch.stored[c.index], 16)
                    if c.index + 2 < len(CHUNKS):
                        sp.wait_ge(ch.stored[c.index], 64)
                        load_x(CHUNKS[c.index + 2])
                for e in range(X):
                    k = s.index * X + e + 2
                    if k < len(SETS) * X:
                        load_weights(k)
            sp.wait_ge(s_zero_rows, 16)
            for done in ch.stored:
                sp.wait_ge(done, 64)

        @block.gpsimd
        def _(pool):
            own = Order(pool, s_pool).own

            def ramp(to, pattern, base=0, step=0):
                own(pool.iota(to, pattern, base=base, channel_multiplier=step, allow_small_or_imprecise_dtypes=True))

            pool.memset(we_f[:, :], 0.0).then_inc(s_edge_zero, 1)
            own(pool.memset(ident[:, :], 0.0))
            own(pool.affine_select(out=ident[:, :], in_=ident[:, :], compare_op=ALU.not_equal, fill=1.0,
                                   base=0, pattern=[[-1, 128]], channel_multiplier=1))
            own(pool.memset(ones[:, :], 1.0))
            own(pool.affine_select(out=tri[:, :], in_=ones[:, :], compare_op=ALU.is_gt, fill=0.0,
                                   base=0, pattern=[[1, 128]], channel_multiplier=-1))
            ramp(iota_w[:, :], [[1, 128]])
            ramp(iota_x[:, :], [[1, X]])
            ramp(iota_mx[:, :], [[1, X]], base=-X)
            ramp(thr[:, :, :], [[0, X], [T, TPE]])
            ramp(thr_w[:, :], [[WIN, NWIN]])
            ramp(pad_i[:, :], [[128, TH]], base=N, step=1)
            for s in SETS:
                ramp(pad_row[s.index][:, :], [[0, NH // TH], [128, TH]], base=N + 1 - s.chunks[0].first, step=1)
                for c in s.chunks:
                    ramp(node1[s.index][:, c.a - s.first_block:c.z - s.first_block], [[1, c.blocks]],
                         base=c.first - s.chunks[0].first + 1, step=c.blocks)
                own(pool.memset(slot_read[s.index][:, :], 0))
                own(pool.memset(slot_add[s.index][:, :], 0))
                own(pool.memset(slot_w[s.index][:, :], 0.0))
            for t in (rel_t, src_t, ew_t):
                own(pool.memset(t[:, NG:2 * UMAX, :], 0))
            own(pool.memset(base_r[:, NG:2 * UMAX], 0.0))
            for c in CHUNKS[:-1]:
                own(pool.memset(chunk_end[:, c.index:c.index + 1], float(c.first + c.nodes)))
            for i in range(REST + 1):
                own(pool.memset(cut_lo[:, i:i + 1], float(NP - REST + i if i else 0)))
            for k in range(2):
                own(pool.memset(scan[k][:, 0:SHB, :], 0.0))
                own(pool.memset(scx[k][:, 0:SHX], 0.0))
            own(pool.memset(zeros[:, :, :], 0.0))
            own(pool.memset(acc[:, :, :], 0.0))
            pool.sem_inc(s_const, 1)

            def gather_pair(q, u):
                for h in range(RING // 2):
                    pool.wait_ge(q.idx, u * (RING // 2) + h + 1)
                    pool.sem_inc(s_go, 1)
                    for k in (2 * h, 2 * h + 1):
                        pool.indirect_dma_start(G[:, k, :], None, xn_d,
                                                bass.IndirectOffsetOnAxis(idx_ring[:, k:k + 1], 0)).then_inc(q.gathered[k], 16)

            pool.wait_ge(s_tables, 1)
            n_pre = pool.value_load(before_i[0:1, 0:1], min_val=0, max_val=NWIN)
            pool.wait_ge(s_xn_rows, 32 * NC)
            with pool.If(n_pre):
                with pool.Fori(0, n_pre) as ps:
                    with pool.Fori(0, NP) as i:
                        gather_pair(pre, ps * NP + i)
                pool.wait_ge(pre.acc, n_pre * NG + 2)
            with pool.Fori(0, U0 + 1) as u:
                gather_pair(main, u)

            for s, q in zip(SETS, sems):
                k = s.index
                if k == 0:
                    own(pool.memset(ost[:, :, :], 0.0))
                pool.wait_ge(s_zero_rows, 16)
                for h in range(TH):
                    pool.indirect_dma_start(out, bass.IndirectOffsetOnAxis(pad_i[:, h:h + 1], 0),
                                            zeros[:, h, :], None, compute_op=ALU.add).then_inc(q.added[h], 16)
                pool.wait_ge(q.route, 1)
                for c in s.chunks:
                    pool.wait_ge(ch.stored[c.index], 64)

                def gather(tile, n):
                    pool.tensor_copy(gat_i[:, :], slot_read[k][:, bass.ds(tile * TH, TH)]).then_inc(q.index, 1)
                    pool.wait_ge(q.index, n)
                    pool.sem_inc(s_go, 1)
                    for h in range(TH):
                        pool.indirect_dma_start(yg[:, h, :], None, y_d[k],
                                                bass.IndirectOffsetOnAxis(gat_i[:, h:h + 1], 0)).then_inc(q.tile_in[h], 16)

                gather(0, 1)
                pool.wait_ge(q.tile_t, 1)
                gather(1, 2)
                for e in range(X):
                    first = pool.value_load(starts[k][0:1, e:e + 1], min_val=e, max_val=s.max_tiles - 1)
                    end = pool.value_load(starts[k][0:1, e + 1:e + 2], min_val=e + 1, max_val=s.max_tiles)
                    with pool.Fori(first, end) as g:
                        pool.wait_ge(q.tile_t, g + 2)
                        gather(g + 2, g * 2 + 3)
                        if k == 0:
                            gather_pair(main, g + (U0 + 1))
                        for h in range(TH):
                            pool.wait_ge(q.added[h], (g + 1) * 16)
                        pool.tensor_copy(add_i[:, :], slot_add[k][:, bass.ds(g * TH, TH)]).then_inc(q.index, 1)
                        pool.wait_ge(q.index, g * 2 + 4)
                        pool.wait_ge(q.staged, (g + 1) * TH)
                        pool.sem_inc(s_go, 1)
                        for h in range(TH):
                            pool.indirect_dma_start(out, bass.IndirectOffsetOnAxis(add_i[:, h:h + 1], 0),
                                                    ost[:, h, :], None, compute_op=ALU.add).then_inc(q.added[h], 16)
                for h in range(TH):
                    pool.wait_ge(q.added[h], (end + 1) * 16)
                    pool.wait_ge(q.tile_in[h], (end + 2) * 16)
                if k == 0:
                    pool.sem_inc(s_go, 1)
                    pool.wait_ge(s_cuts, 1)
                    n = pool.value_load(cuts_i[0:1, 1, REST:REST + 1], min_val=0, max_val=NP - 1)
                    with pool.If(n):
                        with pool.Fori(end + (U0 + 1), NP) as u:
                            gather_pair(main, u)

        @block.scalar
        def _(act):
            def root(var, done, waited, a, z):
                act.wait_ge(var, waited)
                nc.scalar.activation(sq[:, a:z], ve[:, a:z], ACT.Sqrt).then_inc(done, 1)

            for c in range(NC + 1):
                if c < NC:
                    root(s_var, s_root, c + 1, c * CB, (c + 1) * CB)
                if c >= 1:
                    act.wait_ge(s_scale, c)
                    for b in range((c - 1) * CB, c * CB):
                        nc.scalar.activation(xn_sb[:, b, :], x_sb[:, b, :], ACT.Identity, bias=nmr[:, b:b + 1],
                                             scale=rstd[:, b:b + 1]).then_inc(s_xn, 1)

            src_v = flat(src_t[:, :, :])

            def numbers(q, u, i):
                for h in range(RING // 2):
                    act.wait_ge(q.used, u * RING + 2 * h + 2)
                    nc.scalar.activation(idx_ring[:, 2 * h:2 * h + 2],
                                         src_v[:, bass.ds(i * RING + 2 * h, 2)], ACT.Copy).then_inc(q.idx, 1)

            def split_high(x, which):
                raw_in, done = ((s_raw1, s_hi1), (s_raw2, s_hi2))[which - 1]
                act.wait_ge(raw_in, 16 * (x + 1))
                for raw, hi, lo in split_steps(x, which):
                    nc.scalar.activation(hi, raw, ACT.Copy).then_inc(done, 1)

            act.wait_ge(s_tables, 1)
            n_pre = act.value_load(before_i[0:1, 0:1], min_val=0, max_val=NWIN)
            with act.If(n_pre):
                with act.Fori(0, n_pre) as ps:
                    with act.Fori(0, NP) as i:
                        numbers(pre, ps * NP + i, i)
                act.wait_ge(pre.acc, n_pre * NG + 2)
                act.sem_inc(s_over, 1)
            numbers(main, 0, 0)
            split_high(0, 1)
            split_high(0, 2)

            def pair(u):
                numbers(main, u + 1, u + 1)

            def pairs(a, z):
                with act.Fori(a, z) as u:
                    pair(u)

            def normalise(c):
                act.wait_ge(ch.scale, c.index + 1)
                if c.index >= 2:
                    act.wait_ge(ch.stored[c.index - 2], 64)
                for b in range(c.a, c.z):
                    place = (slice(None), c.index % 2, b - c.a, slice(None))
                    nc.scalar.activation(yr[place], xr[place], ACT.Identity, bias=nmr[:, b:b + 1],
                                         scale=rstd[:, b:b + 1]).then_inc(ch.y, 1)

            def copy_turned(c):
                for b in range(c.a, c.z):
                    act.wait_ge(ch.yt, b + 1)
                    if b >= 2:
                        act.wait_ge(ch.gate, b - 1)
                    nc.scalar.activation(yt_sb[:, b % 2, :, :],
                                         places[b % 2][:, 0:KD * 128].rearrange("q (k p) -> q k p", p=128)[:, :, 0:P],
                                         ACT.Copy).then_inc(ch.yt_sb, 1)

            def chunk_root(c):
                root(ch.var, ch.root, c.index + 1, c.a, c.z)

            done = 0
            for c in SETS[0].chunks:
                u = COMPLETE[c.index]
                pairs(done, u)
                chunk_root(c)
                pair(u)
                normalise(c)
                pair(u + 1)
                copy_turned(c)
                done = u + 2

            for s, q in zip(SETS, sems):
                k = s.index

                def aside(name):
                    if k == 0:
                        pair(BESIDE[name])

                if k == 1:
                    def rest(i):
                        a, z, n = cut_of(act, i)
                        with act.If(n):
                            pairs(a, z)

                    c0, c1, c2 = s.chunks
                    act.wait_ge(s_cuts, 1)
                    rest(0)
                    chunk_root(c0)
                    rest(1)
                    normalise(c0)
                    rest(2)
                    copy_turned(c0)
                    chunk_root(c1)
                    rest(3)
                    normalise(c1)
                    rest(4)
                    copy_turned(c1)
                    rest(5)
                    chunk_root(c2)
                    normalise(c2)
                    copy_turned(c2)
                act.wait_ge(q.delta, 1)
                nc.scalar.activation(ex[:, 0:s.blocks], dl[:, 0:s.blocks], ACT.Exp).then_inc(q.exp, 1)
                aside("chosen")
                aside("ranked")
                aside("half")

                act.wait_ge(q.route, 1)
                act.wait_ge(s_b1_t, 1)
                for e in range(X):
                    nxt = k * X + e + 1
                    first = act.value_load(starts[k][0:1, e:e + 1], min_val=e, max_val=s.max_tiles - 1)
                    end = act.value_load(starts[k][0:1, e + 1:e + 2], min_val=e + 1, max_val=s.max_tiles)
                    if nxt < len(SETS) * X:
                        if e >= 1:
                            act.wait_ge(q.hidden, first * NQ)
                        split_high(nxt, 1)
                    with act.Fori(first, end) as g:
                        for j in range(NQ):
                            act.wait_ge(q.hidden, g * NQ + j + 1)
                            act.wait_ge(q.h_split, g * NQ + j + 1)
                            for m in range(2):
                                c = 2 * j + m
                                nc.scalar.activation(hf[:, j % 2, m, :], ps_h[:, j % 2, m * T:(m + 1) * T], ACT.Gelu,
                                                     bias=b1_t[:, e * KH + c:e * KH + c + 1]).then_inc(q.gelu, 1)
                        if k == 0:
                            numbers(main, g + (U0 + 1), g + (U0 + 1))
                    if nxt < len(SETS) * X:
                        if e >= 1:
                            act.wait_ge(q.result, first)
                        split_high(nxt, 2)

        @block.tensor
        def _(pe):
            pe.wait_ge(s_const, 1)
            banks = (ps_h[:, 0, :], ps_h[:, 1, :], ps_y[:, :])
            for k, rows in enumerate((e_f, xe_f, we_f)):
                if k < 2:
                    pe.wait_ge(s_rows, k + 1)
                else:
                    pe.wait_ge(s_weights, 32)
                for c in range(GT):
                    last = nc.tensor.transpose(banks[k][:, c * NG:(c + 1) * NG], rows[:, c * 128:(c + 1) * 128],
                                               ident[0:NG, 0:NG])
                last.then_inc(s_cols, 1)
            for k in range(2):
                nc.tensor.transpose(ps_m[0:1, k * 128:k * 128 + NG], base_f[:, 2 * k:2 * k + 1], ident[0:NG, 0:NG])
            pe.wait_ge(s_b1, 16)
            nc.tensor.transpose(ps_b1, b1_in[:, :], ident[0:X * KH, 0:X * KH]).then_inc(s_cols, 1)

            def sum_pair(q, u):
                for j in range(2):
                    pe.wait_ge(q.acc, u * 2 + j + 1)
                    for c in range(GT):
                        k = j * GT + c
                        pe.wait_ge(q.window, u * RING + k + 1)
                        pe.wait_ge(q.gathered[k], (u + 1) * 16)
                        for m in range(KD):
                            last = nc.tensor.matmul(ps_agg[:, j, m * WIN:(m + 1) * WIN],
                                                    G[:, k, m * 128:(m + 1) * 128], S[:, k, :],
                                                    start=(c == 0 and m == 0), stop=(c == GT - 1 and m == KD - 1))
                        last.then_inc(q.used, 1)

            pe.wait_ge(s_tables, 1)
            n_pre = pe.value_load(before_i[0:1, 0:1], min_val=0, max_val=NWIN)
            pe.sem_inc(pre.used, RING)
            pe.sem_inc(main.used, RING)
            with pe.If(n_pre):
                with pe.Fori(0, n_pre) as ps:
                    with pe.Fori(0, NP) as i:
                        sum_pair(pre, ps * NP + i)
                pe.wait_ge(pre.acc, n_pre * NG + 2)

            def pair(u):
                sum_pair(main, u)

            def pairs(a, z):
                with pe.Fori(a, z) as u:
                    pair(u)

            def linear(c):
                pe.wait_ge(main.acc, COMPLETE[c.index] * 2 + 2)
                if c.index:
                    pe.wait_ge(ch.yt_sb, c.a)
                    pe.wait_ge(ch.logits, c.index)
                v = acc[:, :, c.first:c.first + c.nodes].rearrange("q k (p b) -> q k b p", b=c.blocks)
                for b in range(c.a, c.z):
                    if b >= c.a + 2:
                        pe.wait_ge(ch.sum, b - 1)
                    for m in range(KD):
                        last = nc.tensor.matmul(places[b % 2][0:P, 0:D], v[:, m, b - c.a, :], wn_sb[:, m, :],
                                                start=(m == 0), stop=(m == KD - 1))
                    last.then_inc(ch.lin, 1)

            def gate(c, b):
                pe.wait_ge(ch.yt_sb, b + 1)
                for m in range(KD):
                    last = nc.tensor.matmul(ps_gate[:, (b - c.a) * X:(b - c.a + 1) * X], yt_sb[:, b % 2, m, :],
                                            wg_sb[:, m, :], start=(m == 0), stop=(m == KD - 1))
                last.then_inc(ch.gate, 1)

            def turn(c):
                for b in range(c.a, c.z):
                    pe.wait_ge(ch.y, b + 1)
                    if b >= c.a + 2:
                        pe.wait_ge(ch.yt_sb, b - 1)
                    for m in range(KD):
                        last = nc.tensor.transpose(places[b % 2][:, m * 128:m * 128 + P],
                                                   yr[:, c.index % 2, b - c.a, m * 128:(m + 1) * 128], ident[0:P, 0:P])
                    last.then_inc(ch.yt, 1)
                    if b > c.a:
                        gate(c, b - 1)
                gate(c, c.z - 1)

            done = 0
            for c in SETS[0].chunks:
                u = COMPLETE[c.index]
                pairs(done, u)
                if c.index == 0:
                    pe.wait_ge(s_small, 16 * 5)
                linear(c)
                pair(u)
                pair(u + 1)
                turn(c)
                done = u + 2

            for s, q in zip(SETS, sems):
                k, B = s.index, s.blocks

                def aside(name):
                    if k == 0:
                        pair(BESIDE[name])

                if k == 1:
                    def rest(i):
                        a, z, n = cut_of(pe, i)
                        with pe.If(n):
                            pairs(a, z)

                    c0, c1, c2 = s.chunks
                    pe.wait_ge(sems[0].biased, end + 1)
                    pe.wait_ge(sems[0].y_split, end + 1)
                    pe.sem_inc(s_over, 1)
                    pe.wait_ge(s_cuts, 1)
                    rest(0)
                    linear(c0)
                    rest(1)
                    rest(2)
                    turn(c0)
                    linear(c1)
                    rest(3)
                    rest(4)
                    turn(c1)
                    rest(5)
                    linear(c2)
                    turn(c2)

                pe.wait_ge(q.mask, 1)
                mk = flat(mask[:, 0:B, :])
                nc.tensor.matmul(ps_o[0:P, 0, 0:B * X], tri[0:P, 0:P], mk, start=True, stop=True)
                nc.tensor.matmul(ps_o[0:P, 1, 0:B * X], ones[0:P, 0:P], mk, start=True, stop=True).then_inc(q.rank, 1)
                aside("chosen")
                aside("ranked")
                ps_inv = ps_m[:, 0:2 * NH]
                for n, (lo, hi) in enumerate(steps_of(B)):
                    pe.wait_ge(q.onehot, 3 * n + 3)
                    for j in range(2):
                        for b in range(hi - lo):
                            last = nc.tensor.matmul(ps_inv, oh_lo[:, n % 2, j, b, :],
                                                    oh_hi[:, n % 2, j, b, :, :].rearrange("p a h -> p (a h)"),
                                                    start=(n == 0 and j == 0 and b == 0),
                                                    stop=(hi == B and j == 1 and b == hi - lo - 1))
                    last.then_inc(q.onehot_used, 1)
                    if n == 1:
                        aside("half")

                def transpose_tile(n):
                    for h in range(TH):
                        pe.wait_ge(q.tile_in[h], n * 16)
                    for h in range(TH):
                        for m in range(KD):
                            last = nc.tensor.transpose(ps_y[:, m * T + h * 128:m * T + (h + 1) * 128],
                                                       yg[:, h, m * 128:(m + 1) * 128], ident[:, :])
                    last.then_inc(q.tile_t, 1)

                pe.wait_ge(q.route, 1)
                transpose_tile(1)
                pe.sem_inc(q.biased, 1)
                pe.sem_inc(q.gelu, 4)
                pe.sem_inc(q.h_split, 2)
                for e in range(X):
                    cur = k * X + e
                    w1_hi, w1_lo, w2_hi, w2_lo = parts[cur % 2]
                    first = pe.value_load(starts[k][0:1, e:e + 1], min_val=e, max_val=s.max_tiles - 1)
                    end = pe.value_load(starts[k][0:1, e + 1:e + 2], min_val=e + 1, max_val=s.max_tiles)
                    pe.wait_ge(s_split1, STEPS * (cur + 1))
                    with pe.Fori(first, end) as g:
                        pe.wait_ge(q.y_split, g + 1)
                        for j in range(NQ):
                            pe.wait_ge(q.gelu, (g * NQ + j) * 2 + 2)
                            for m2_ in range(2):
                                c = 2 * j + m2_
                                terms = [(m, a, b) for m in range(KD) for a, b in
                                         ((w1_hi, y_hi), (w1_hi, y_lo), (w1_lo, y_hi))]
                                for n, (m, a, b) in enumerate(terms):
                                    last = nc.tensor.matmul(ps_h[:, j % 2, m2_ * T:(m2_ + 1) * T],
                                                            a[:, m, c * 128:(c + 1) * 128], b[:, m, :],
                                                            start=(n == 0), stop=(n == len(terms) - 1))
                            last.then_inc(q.hidden, 1)
                        transpose_tile(g + 2)
                        if k == 0:
                            sum_pair(main, g + U0)
                        pe.wait_ge(q.biased, g + 1)
                        pe.wait_ge(s_split2, STEPS * (cur + 1))
                        for j in range(NQ):
                            pe.wait_ge(q.h_split, g * NQ + j + 3)
                            for c in (2 * j, 2 * j + 1):
                                for n, (a, b) in enumerate(((h_hi, w2_hi), (h_hi, w2_lo), (h_lo, w2_hi))):
                                    for h in range(TH):
                                        last = nc.tensor.matmul(ps_o[:, h, 0:D], a[:, c, h * 128:(h + 1) * 128],
                                                                b[:, c, :], start=(c == 0 and n == 0),
                                                                stop=(c == KH - 1 and n == 2))
                        last.then_inc(q.result, 1)

        @block.vector
        def _(dve):
            order = Order(dve, s_dve)
            own, mark, need = order.own, order.mark, order.need
            V = nc.vector

            def stats(blocks, rows, make=None, var=None):
                n, made, seen = len(blocks), [], []
                for t in range(n + 2):
                    if t < n and make:
                        made.append(make(blocks[t]))
                    if 1 <= t <= n:
                        b = blocks[t - 1]
                        if make:
                            need(made[t - 1])
                        seen.append(mark(V.bn_stats(bn[:, b, :], rows(b))))
                    if t >= 2:
                        b = blocks[t - 2]
                        need(seen[t - 2])
                        last = mark(V.bn_aggr(mv[:, b, :], bn[:, b, :]))
                need(last)
                a, z = blocks[0], blocks[-1] + 1
                V.tensor_scalar(ve[:, a:z], mv[:, a:z, 1], EPS, None, ALU.add).then_inc(var, 1)

            def scales(roots, done, waited, a, z):
                dve.wait_ge(roots, waited)
                own(V.reciprocal(nwt[:, a:z], sq[:, a:z]))
                own(V.tensor_tensor(nwt[:, a:z], nwt[:, a:z], ve[:, a:z], ALU.mult))
                own(V.tensor_tensor(nwt[:, a:z], nwt[:, a:z], sq[:, a:z], ALU.add))
                own(V.tensor_scalar(nwt[:, a:z], nwt[:, a:z], 0.5, None, ALU.mult))
                own(V.reciprocal(rstd[:, a:z], nwt[:, a:z]))
                V.scalar_tensor_tensor(out=nmr[:, a:z], in0=mv[:, a:z, 0], scalar=-1.0, in1=rstd[:, a:z],
                                       op0=ALU.mult, op1=ALU.mult).then_inc(done, 1)

            for c in range(NC + 1):
                if c < NC:
                    dve.wait_ge(s_x[c], 32)
                    stats(range(c * CB, (c + 1) * CB), lambda b: x_sb[:, b, :], var=s_var)
                if c >= 1:
                    scales(s_root, s_scale, c, (c - 1) * CB, c * CB)

            dve.wait_ge(s_dst, 48)
            own(V.tensor_copy(e_f[:, :], e_int[:, :]))
            own(V.tensor_reduce(base_f[:, 0:1], e_f[:, :], AX.X, ALU.min))
            n_max = mark(V.tensor_reduce(base_f[:, 1:2], e_f[:, :], AX.X, ALU.max))
            dve.wait_ge(s_src, 48)
            V.tensor_copy(xe_f[:, :], xe_int[:, :])
            need(n_max)
            own(V.tensor_tensor(base_f[:, 2:3], base_f[:, 1:2], base_f[:, 0:1], ALU.subtract))
            own(V.tensor_scalar(e_f[:, :], e_f[:, :], base_f[:, 0:1], None, ALU.subtract))
            dve.sem_inc(s_rows, 2)
            dve.wait_ge(s_const, 1)
            banks = (ps_h[:, 0, :], ps_h[:, 1, :], ps_y[:, :])
            for k, to in enumerate((rel_t, src_t, ew_t)):
                dve.wait_ge(s_cols, k + 1)
                V.tensor_copy(to[:, 0:NG, :], banks[k][:, 0:GT * NG].rearrange("p (c g) -> p g c", g=NG))
            dve.wait_ge(s_cols, 4)
            own(V.tensor_copy(base_r[:, 0:NG], ps_m[0:1, 0:NG]))
            V.tensor_copy(b1_t[:, :], ps_b1).then_inc(s_b1_t, 1)
            own(V.tensor_reduce(span[:, 0:1], ps_m[0:1, 128:128 + NG], AX.X, ALU.max))
            V.tensor_copy(base_i[:, :], base_r[:, :])
            own(V.tensor_scalar(span[:, 4:4 + NWIN], thr_w[:, :], span[:, 0:1], None, ALU.is_le))
            own(V.tensor_reduce(span[:, 1:2], span[:, 4:4 + NWIN], AX.X, ALU.add))
            for c in CHUNKS[:-1]:
                n = mark(V.tensor_reduce(least[:, 0, c.index:c.index + 1], base_r[:, 2 * COMPLETE[c.index]:NG], AX.X, ALU.min))
            need(n)
            own(V.tensor_tensor(least[:, 1, :], least[:, 0, :], chunk_end[:, :], ALU.is_lt))
            own(V.tensor_reduce(span[:, 2:3], least[:, 1, :], AX.X, ALU.max))
            own(V.tensor_scalar(span[:, 3:4], span[:, 1:2], 1.0, None, ALU.is_gt))
            own(V.tensor_tensor(span[:, 2:3], span[:, 2:3], span[:, 3:4], ALU.max))
            own(V.tensor_tensor(span[:, 2:3], span[:, 2:3], span[:, 1:2], ALU.mult))
            own(V.tensor_copy(before_i[:, :], span[:, 2:3]))
            dve.sem_inc(s_tables, 1)

            rel_v, ew_v = flat(rel_t[:, :, :]), flat(ew_t[:, :, :])

            def windows(q, u, i, j):
                dve.wait_ge(q.used, u * RING + (j + 1) * GT)
                for k in range(j * GT, (j + 1) * GT):
                    t = bass.ds(i * RING + k, 1)
                    V.tensor_scalar(S[:, k, :], iota_w[:, 0:WIN], rel_v[:, t], ew_v[:, t],
                                    ALU.is_equal, ALU.mult).then_inc(q.window, 1)

            def add_group(q, u, i, j):
                base = dve.value_load(base_i[0:1, bass.ds(i * 2 + j, 1)], min_val=0, max_val=N)
                dve.wait_ge(q.used, (u + 1) * RING + (j + 1) * GT)
                dve.wait_ge(q.acc, u * 2 + j + 2)
                to = acc[:, :, bass.ds(base, WIN)]
                V.tensor_tensor(to, to, ps_agg[:, j, 0:KD * WIN].rearrange("q (k w) -> q k w", k=KD),
                                ALU.add).then_inc(q.acc, 1)

            def split_low(x, which):
                high, done = ((s_hi1, s_split1), (s_hi2, s_split2))[which - 1]
                for n, (raw, hi, lo) in enumerate(split_steps(x, which)):
                    dve.wait_ge(high, STEPS * x + n + 1)
                    V.tensor_tensor(lo, raw, hi.bitcast(f32), ALU.subtract).then_inc(done, 1)

            dve.sem_inc(pre.acc, 2)
            dve.sem_inc(main.acc, 2)
            n_pre = dve.value_load(before_i[0:1, 0:1], min_val=0, max_val=NWIN)
            with dve.If(n_pre):
                with dve.Fori(0, n_pre) as ps:
                    with dve.Fori(0, NP) as i:
                        for j in range(2):
                            windows(pre, ps * NP + i, i, j)
                        for j in range(2):
                            add_group(pre, ps * NP + i, i, j)
                    V.tensor_scalar(rel_v, rel_v, float(-WIN), None, ALU.add).then_inc(s_next, 1)
                    V.tensor_scalar(base_r[:, :], base_r[:, :], float(WIN), float(N), ALU.add, ALU.min).then_inc(s_next, 1)
                    dve.wait_ge(s_next, ps * 3 + 2)
                    V.tensor_copy(base_i[:, :], base_r[:, :]).then_inc(s_next, 1)
                    dve.wait_ge(s_next, ps * 3 + 3)
                dve.wait_ge(pre.acc, n_pre * NG + 2)
                V.memset(ew_v, 0.0).then_inc(s_next, 1)
                dve.wait_ge(s_next, n_pre * 3 + 1)
                dve.sem_inc(s_over, 1)
            for j in range(2):
                windows(main, 0, 0, j)
            split_low(0, 1)
            split_low(0, 2)

            def pair(u):
                for j in range(2):
                    add_group(main, u, u, j)
                    windows(main, u + 1, u + 1, j)

            def pairs(a, z):
                with dve.Fori(a, z) as u:
                    pair(u)

            def bias(c):
                dve.wait_ge(ch.x[c.index], 32)
                place = xr[:, c.index % 2, 0:c.blocks, :]
                own(V.tensor_tensor(place, place, bias_bc[0:P, :].unsqueeze(1).to_broadcast([P, c.blocks, D]), ALU.add))

            def residual(c):
                seen = []
                for b in range(c.a, c.z + 2):
                    if b < c.z:
                        dve.wait_ge(ch.lin, b + 1)
                        place = xr[:, c.index % 2, b - c.a, :]
                        V.tensor_tensor(place, places[b % 2][0:P, 0:D], place, ALU.add).then_inc(ch.sum, 1)
                    if c.a < b <= c.z:
                        dve.wait_ge(ch.sum, b)
                        seen.append(mark(V.bn_stats(bn[:, b - 1, :], xr[:, c.index % 2, b - 1 - c.a, :])))
                    if b >= c.a + 2:
                        need(seen[b - 2 - c.a])
                        last = mark(V.bn_aggr(mv[:, b - 2, :], bn[:, b - 2, :]))
                need(last)
                V.tensor_scalar(ve[:, c.a:c.z], mv[:, c.a:c.z, 1], EPS, None, ALU.add).then_inc(ch.var, 1)

            def chunk_scales(c):
                scales(ch.root, ch.scale, c.index + 1, c.a, c.z)

            def logits(c):
                dve.wait_ge(ch.gate, c.z)
                b0 = SETS[c.index >= L0].first_block
                V.tensor_tensor(lg[:, c.a - b0:c.z - b0, :],
                                ps_gate[:, 0:c.blocks * X].rearrange("p (b e) -> p b e", e=X),
                                bg_bc[0:P, :].unsqueeze(1).to_broadcast([P, c.blocks, X]), ALU.add).then_inc(ch.logits, 1)

            done = 0
            for c in SETS[0].chunks:
                u = COMPLETE[c.index]
                pairs(done, u)
                if c.index == 0:
                    dve.wait_ge(s_small, 16 * 5)
                    bias(c)
                residual(c)
                pair(u)
                chunk_scales(c)
                pair(u + 1)
                logits(c)
                if c.index + 1 < L0:
                    bias(CHUNKS[c.index + 1])
                done = u + 2

            for s, q in zip(SETS, sems):
                k, B = s.index, s.blocks

                def aside(name):
                    if k == 0:
                        pair(BESIDE[name])

                if k == 1:
                    def rest(i):
                        a, z, n = cut_of(dve, i)
                        with dve.If(n):
                            pairs(a, z)

                    own(V.tensor_scalar(cuts[:, 2, 0:1], starts[0][:, X:X + 1], float(U0), None, ALU.add))
                    own(V.tensor_scalar(cuts[:, 0, :], cut_lo[:, :], cuts[:, 2, 0:1], None, ALU.max))
                    own(V.tensor_tensor(cuts[:, 1, 0:REST], cuts[:, 0, 1:REST + 1], cuts[:, 0, 0:REST], ALU.subtract))
                    own(V.tensor_scalar(cuts[:, 1, REST:REST + 1], cuts[:, 2, 0:1], -1.0, float(NP - 1), ALU.mult, ALU.add))
                    own(V.tensor_scalar(cuts[:, 1, REST:REST + 1], cuts[:, 1, REST:REST + 1], 0.0, None, ALU.max))
                    own(V.tensor_copy(cuts_i[:, :, :], cuts[:, 0:2, :]))
                    dve.sem_inc(s_cuts, 1)
                    c0, c1, c2 = s.chunks
                    bias(c0)
                    rest(0)
                    residual(c0)
                    rest(1)
                    chunk_scales(c0)
                    rest(2)
                    logits(c0)
                    bias(c1)
                    residual(c1)
                    rest(3)
                    chunk_scales(c1)
                    rest(4)
                    logits(c1)
                    bias(c2)
                    rest(5)
                    residual(c2)
                    chunk_scales(c2)
                    logits(c2)
                dve.wait_ge(ch.logits, s.chunks[-1].index + 1)

                def cut(a):
                    return a[:, 0:B, :] if len(a.shape) == 3 else a[:, 0:B]

                def bc(a):
                    return a.unsqueeze(2).to_broadcast([P, B, X])

                def bx(a):
                    return a.unsqueeze(1).to_broadcast([P, B, X])

                def per_block(a):
                    return a.rearrange("p (b e) -> p b e", e=X)

                def choose(logit, m, i, oh):
                    own(V.tensor_reduce(cut(m), cut(logit), AX.X, ALU.max))
                    own(V.tensor_tensor(cut(cand), cut(logit), bc(cut(m)), ALU.is_equal))
                    own(V.scalar_tensor_tensor(out=cut(cand), in0=cut(cand), scalar=float(-X), in1=bx(iota_x[0:P, :]),
                                               op0=ALU.mult, op1=ALU.add))
                    own(V.tensor_reduce(cut(i), cut(cand), AX.X, ALU.min))
                    own(V.tensor_tensor(cut(oh), bx(iota_mx[0:P, :]), bc(cut(i)), ALU.is_equal))

                choose(lg, m1, i1, oh1)
                own(V.scalar_tensor_tensor(out=cut(lg2), in0=cut(oh1), scalar=NEG, in1=cut(lg), op0=ALU.mult, op1=ALU.add))
                choose(lg2, m2, i2, oh2)
                V.tensor_tensor(cut(mask), cut(oh1), cut(oh2), ALU.add).then_inc(q.mask, 1)
                V.tensor_tensor(cut(dl), cut(m2), cut(m1), ALU.subtract).then_inc(q.delta, 1)
                aside("chosen")

                dve.wait_ge(q.rank, 1)
                ps_rank, ps_tot = per_block(ps_o[0:P, 0, 0:B * X]), per_block(ps_o[0:P, 1, 0:B * X])
                V.tensor_copy(cut(tot), ps_tot)
                own(V.tensor_copy(scan[0][:, SHB:SHB + B, :], ps_tot))
                cur, step = 0, 1
                while step < B:
                    a, b = scan[cur], scan[1 - cur]
                    own(V.tensor_tensor(b[:, SHB:SHB + B, :], a[:, SHB:SHB + B, :], a[:, SHB - step:SHB + B - step, :], ALU.add))
                    cur, step = 1 - cur, step * 2
                run = scan[cur]
                dve.wait_ge(q.exp, 1)
                n_den = mark(V.tensor_scalar(cut(dl), cut(ex), 1.0, None, ALU.add))
                chosen = run[:, SHB + B - 1, :]
                own(V.tensor_tensor(cmp[:, :, :], thr[0:P, :, :], chosen.unsqueeze(2).to_broadcast([P, X, TPE]), ALU.is_lt))
                n_w1 = mark(V.reciprocal(gw[:, 0, 0:B], cut(dl)))
                own(V.tensor_reduce(tl[:, :], cmp[:, :, :], AX.X, ALU.add))
                V.tensor_tensor(gw[:, 1, 0:B], cut(ex), gw[:, 0, 0:B], ALU.mult)
                own(V.tensor_scalar(scx[0][:, SHX:SHX + X], tl[:, :], 1.0, None, ALU.max))
                own(V.tensor_tensor(cut(slotpos), run[:, SHB:SHB + B, :], cut(tot), ALU.subtract))
                cx, step = 0, 1
                while step < X:
                    a, b = scx[cx], scx[1 - cx]
                    own(V.tensor_tensor(b[:, SHX:SHX + X], a[:, SHX:SHX + X], a[:, SHX - step:SHX + X - step], ALU.add))
                    cx, step = 1 - cx, step * 2
                before = scx[cx][:, SHX - 1:SHX + X - 1]
                V.tensor_copy(starts[k][:, :], scx[cx][0:1, SHX - 1:SHX + X])
                own(V.tensor_tensor(cut(slotpos), cut(slotpos), ps_rank, ALU.add))
                own(V.scalar_tensor_tensor(out=cut(slotpos), in0=bx(before), scalar=float(T), in1=cut(slotpos),
                                           op0=ALU.mult, op1=ALU.add))
                own(V.tensor_tensor(cut(prod), cut(oh1), cut(slotpos), ALU.mult))
                n_p = mark(V.tensor_tensor(cut(cand), cut(oh2), cut(slotpos), ALU.mult))
                V.tensor_reduce(pos[:, 0, 0:B], cut(prod), AX.X, ALU.add)
                need(n_p)
                own(V.tensor_reduce(pos[:, 1, 0:B], cut(cand), AX.X, ALU.add))
                own(V.tensor_copy(pos_i[:, :, 0:B], pos[:, :, 0:B]))
                V.tensor_scalar(hi_i[:, :, 0:B], pos_i[:, :, 0:B], 7, None, ALU.arith_shift_right)
                own(V.tensor_scalar(lo_i[:, :, 0:B], pos_i[:, :, 0:B], 127, None, ALU.bitwise_and))
                V.tensor_copy(hi_f[:, :, 0:B], hi_i[:, :, 0:B])
                own(V.tensor_copy(lo_f[:, :, 0:B], lo_i[:, :, 0:B]))
                aside("ranked")
                for n, (lo, hi) in enumerate(steps_of(B)):
                    if n >= 2:
                        dve.wait_ge(q.onehot_used, n - 1)
                    bs, shape = slice(lo, hi), (P, 2, hi - lo)

                    def bj(a, width):
                        return a.unsqueeze(3).to_broadcast([*shape, width])

                    def ramp(width):
                        return iota_w[0:P, 0:width].unsqueeze(1).unsqueeze(1).to_broadcast([*shape, width])

                    place = oh_hi[:, n % 2, :, 0:hi - lo, :, :]
                    n_eq = mark(V.tensor_tensor(place[:, :, :, 1, :], ramp(NH), bj(hi_f[:, :, bs], NH), ALU.is_equal))
                    V.tensor_tensor(oh_lo[:, n % 2, :, 0:hi - lo, :], ramp(128), bj(lo_f[:, :, bs], 128),
                                    ALU.is_equal).then_inc(q.onehot, 1)
                    need(n_eq)
                    V.tensor_tensor(place[:, :, :, 0, :], place[:, :, :, 1, :],
                                    node1[k][0:P, bs].unsqueeze(1).unsqueeze(3).to_broadcast([*shape, NH]),
                                    ALU.mult).then_inc(q.onehot, 1)
                    V.tensor_tensor(place[:, :, :, 1, :], place[:, :, :, 1, :], bj(gw[:, :, bs], NH),
                                    ALU.mult).then_inc(q.onehot, 1)
                    if n == 1:
                        aside("half")
                dve.wait_ge(q.onehot_used, len(steps_of(B)))
                own(V.scalar_tensor_tensor(out=padz[:, :], in0=ps_m[:, 0:NH], scalar=0.0, in1=pad_row[k][:, :],
                                           op0=ALU.is_equal, op1=ALU.mult))
                V.tensor_copy(slot_w[k][:, 0:NH], ps_m[:, NH:2 * NH])
                V.tensor_scalar(slot_read[k][:, 0:NH], ps_m[:, 0:NH], -1.0, 0.0, ALU.add, ALU.max)
                own(V.scalar_tensor_tensor(out=slot_add[k][:, 0:NH], in0=padz[:, :], scalar=float(s.chunks[0].first - 1),
                                           in1=ps_m[:, 0:NH], op0=ALU.add, op1=ALU.add))
                dve.sem_inc(q.route, 1)

                def split_tile(n):
                    t = flat(y_hi[:, :, :])
                    dve.wait_ge(q.tile_t, n)
                    V.tensor_copy(t, ps_y[:, :]).then_inc(q.y_hi, 1)
                    dve.wait_ge(q.y_hi, n)
                    V.tensor_tensor(flat(y_lo[:, :, :]), ps_y[:, :], t.bitcast(f32), ALU.subtract).then_inc(q.y_split, 1)

                split_tile(1)
                for e in range(X):
                    nxt = k * X + e + 1
                    first = dve.value_load(starts[k][0:1, e:e + 1], min_val=e, max_val=s.max_tiles - 1)
                    end = dve.value_load(starts[k][0:1, e + 1:e + 2], min_val=e + 1, max_val=s.max_tiles)
                    if nxt < len(SETS) * X:
                        split_low(nxt, 1)
                    with dve.Fori(first, end) as g:
                        for j in range(NQ):
                            h_in = hf[:, j % 2, :, :]
                            js = slice(2 * j, 2 * j + 2)
                            dve.wait_ge(q.gelu, (g * NQ + j) * 2 + 6)
                            V.tensor_copy(h_hi[:, js, :], h_in).then_inc(q.h_hi, 1)
                            dve.wait_ge(q.h_hi, g * NQ + j + 1)
                            V.tensor_tensor(h_lo[:, js, :], h_in, h_hi[:, js, :].bitcast(f32),
                                            ALU.subtract).then_inc(q.h_split, 1)
                        split_tile(g + 2)
                        if k == 0:
                            pair(g + U0)
                        dve.wait_ge(q.result, g + 1)
                        for h in range(TH):
                            dve.wait_ge(q.added[h], (g + 1) * 16)
                        V.tensor_tensor(ost[:, :, :], ps_o[:, :, 0:D],
                                        b2_bc[:, e, :].unsqueeze(1).to_broadcast([128, TH, D]), ALU.add).then_inc(q.biased, 1)
                        dve.wait_ge(q.biased, g + 2)
                        for h in range(TH):
                            V.tensor_scalar(ost[:, h, :], ost[:, h, :], slot_w[k][:, bass.ds(g * TH + h, 1)], None,
                                            ALU.mult).then_inc(q.staged, 1)
                    if nxt < len(SETS) * X:
                        split_low(nxt, 2)


_INS = ["x", "src", "dst", "edge_weight", "L0_gnn_weight", "L0_gnn_bias", "L0_ffn_Wg", "L0_ffn_bg",
        "L0_ffn_W1", "L0_ffn_b1", "L0_ffn_W2", "L0_ffn_b2"]


def kernel(**inputs):
    import numpy as np
    import concourse.bacc as bacc
    from concourse.bass_utils import run_bass_kernel_spmd

    nc = bacc.Bacc("TRN2", target_bir_lowering=False, num_devices=1)
    arrays, args = {}, []
    for name in _INS:
        a = np.ascontiguousarray(inputs[name])
        arrays[f"in_{name}"] = a
        args.append(nc.dram_tensor(f"in_{name}", a.shape, mybir.dt.from_np(a.dtype), kind="ExternalInput").ap())
    nodes, features = inputs["x"].shape
    args.append(nc.dram_tensor("result", (nodes + PAD_ROWS, features), mybir.dt.float32, kind="ExternalOutput").ap())
    gnn_moe_layer(nc, *args)
    run = run_bass_kernel_spmd(nc, [arrays], core_ids=[0])
    return run.results[0]["result"][:nodes]
```

```python
import concourse.bass as bass
from concourse import mybir
from contextlib import ExitStack

PAD_ROWS = 256
CHUNK_BLOCKS = ((4, 4, 3, 2), (5, 4, 3))


class Order:

    def __init__(self, eng, sem):
        self.eng, self.sem, self.n = eng, sem, 0

    def mark(self, ins):
        self.n += 1
        ins.then_inc(self.sem, 1)
        return self.n

    def need(self, n):
        self.eng.wait_ge(self.sem, n)

    def own(self, ins):
        self.need(self.mark(ins))


class EdgeSems:

    def __init__(self, sem, name, ring):
        self.idx = sem(f"s_{name}_idx")
        self.window = sem(f"s_{name}_window")
        self.used = sem(f"s_{name}_used")
        self.acc = sem(f"s_{name}_acc")
        self.gathered = [sem(f"s_{name}_gathered{k}") for k in range(ring)]


class Chunk:

    def __init__(self, index, first_block, blocks, rows):
        self.index, self.first, self.blocks, self.nodes = index, first_block * rows, blocks, blocks * rows
        self.a, self.z = first_block, first_block + blocks


class NodeSet:

    def __init__(self, index, chunks, tile, experts):
        self.index, self.chunks = index, chunks
        self.first_block, self.blocks = chunks[0].a, chunks[-1].z - chunks[0].a
        self.nodes = sum(c.nodes for c in chunks)
        self.max_tiles = (2 * self.nodes - experts) // tile + experts


class ChunkSems:

    def __init__(self, sem, chunks):
        self.x = [sem(f"s_chunk_x{c.index}") for c in chunks]
        self.stored = [sem(f"s_stored{c.index}") for c in chunks]
        self.lin, self.sum, self.var, self.root, self.scale = (
            sem(f"s_{n}") for n in ("lin", "sum", "chunk_var", "chunk_root", "chunk_scale"))
        self.y, self.yt, self.yt_sb, self.gate, self.logits = (
            sem(f"s_{n}") for n in ("y", "yt", "yt_sb", "gate", "logits"))


class SetSems:

    def __init__(self, sem, s, halves):
        def own(what):
            return sem(f"s{s.index}_{what}")

        self.delta, self.exp, self.mask, self.rank = map(own, ("delta", "exp", "mask", "rank"))
        self.onehot, self.onehot_used, self.route = map(own, ("onehot", "onehot_used", "route"))
        self.tile_in = [own(f"tile_in{h}") for h in range(halves)]
        self.tile_t, self.y_hi, self.y_split = map(own, ("tile_t", "y_hi", "y_split"))
        self.hidden, self.gelu, self.h_hi, self.h_split = map(own, ("hidden", "gelu", "h_hi", "h_split"))
        self.result, self.biased, self.staged, self.index = map(own, ("result", "biased", "staged", "index"))
        self.added = [own(f"added{h}") for h in range(halves)]


def gnn_moe_layer(nc, x, src, dst, edge_w, w_gnn, b_gnn, w_gate, b_gate, w1, b1, w2, b2, out):
    f32, f32r, i32 = mybir.dt.float32, mybir.dt.float32r, mybir.dt.int32
    ACT, ALU, AX = mybir.ActivationFunctionType, mybir.AluOpType, mybir.AxisListType

    N, D = x.shape
    E = src.shape[0]
    X = w_gate.shape[1]
    H = w1.shape[2]
    KD, KH = D // 128, H // 128
    EPS = 1e-5
    NEG = -3.0e38

    P, NB, CB = 125, 25, 5
    NC = NB // CB
    assert P * NB == N
    PA = 112

    T = 256
    TH = T // 128
    NQ = KH // 2
    SC = 1024
    STEPS = KD * H // SC
    assert PAD_ROWS == T and KD * H == KH * D

    GT, WIN = 4, 64
    GE = GT * 128
    NG = -(-E // GE)
    NP = NG // 2
    RING = 2 * GT
    assert NP * 2 == NG
    LAST = E - (NG - 1) * GE
    NWIN = -(-N // WIN)

    CHUNKS = []
    for n in CHUNK_BLOCKS[0] + CHUNK_BLOCKS[1]:
        CHUNKS.append(Chunk(len(CHUNKS), CHUNKS[-1].z if CHUNKS else 0, n, P))
    L0 = len(CHUNK_BLOCKS[0])
    SETS = [NodeSet(0, CHUNKS[:L0], T, X), NodeSet(1, CHUNKS[L0:], T, X)]
    BM = max(s.blocks for s in SETS)
    CM = max(c.blocks for c in CHUNKS)
    NH = TH * max(s.max_tiles for s in SETS)
    NHP = NH + 2 * TH
    TPE = -(-max(s.nodes for s in SETS) // T)
    assert CHUNKS[-1].z == NB
    RB = 3

    MORE = 369
    COMPLETE = [-(-((c.first + c.nodes) * E // N + MORE) // (2 * GE)) for c in CHUNKS[:-1]] + [NP]
    DURING = 5
    U0 = COMPLETE[L0 - 1] + DURING
    UMAX = max(U0 + SETS[0].max_tiles, NP) + 2
    REST = 6
    assert NP - REST + 1 >= COMPLETE[-2]

    xn_d = nc.dram_tensor("xn_d", (N, D), f32, kind="Internal").ap()
    y_d = [nc.dram_tensor(f"y{s.index}_d", (s.nodes, D), f32, kind="Internal").ap() for s in SETS]

    def by_partition(a, blocks):
        return a.rearrange("(p b) d -> p b d", b=blocks)

    def of_chunk(a, c, first=0):
        return by_partition(a[c.first - first:c.first - first + c.nodes, :], c.blocks)

    def flat(a):
        return a.rearrange("p a b -> p (a b)")

    SPANS = ((0, PA), (PA, P))

    with ExitStack() as ctx:
        def sb(name, shape, dt=f32, stack=ctx):
            return stack.enter_context(nc.sbuf_tensor(name, shape, dt))

        def pb(name, shape):
            return ctx.enter_context(nc.psum_tensor(name, shape, f32))

        def sem(name):
            return ctx.enter_context(nc.semaphore(name))

        ident = sb("ident", [128, 128])
        iota_w = sb("iota_w", [128, 128])
        iota_x = sb("iota_x", [128, X])
        iota_mx = sb("iota_mx", [128, X])
        tri = sb("tri", [128, 128])
        ones = sb("ones", [128, 128])
        zeros = sb("zeros", [128, PAD_ROWS // 128, D])
        thr = sb("thr", [128, X, TPE])
        thr_w = sb("thr_w", [1, NWIN])
        pad_i = sb("pad_i", [128, TH], i32)
        pad_row = [sb(f"pad_row{s.index}", [128, NH]) for s in SETS]
        node1 = [sb(f"node1_{s.index}", [128, s.blocks]) for s in SETS]
        chunk_end = sb("chunk_end", [1, len(CHUNKS) - 1])
        bias_bc = sb("bias_bc", [128, D])
        bg_bc = sb("bg_bc", [128, X])
        wg_sb = sb("wg_sb", [128, KD, X])
        wn_sb = sb("wn_sb", [128, KD, D])
        b1_in = sb("b1_in", [X * KH, 128])
        b1_t = sb("b1_t", [128, X * KH])
        b2_bc = sb("b2_bc", [128, X, D])

        rel_t = sb("rel_t", [128, 2 * UMAX, GT])
        src_t = sb("src_t", [128, 2 * UMAX, GT], i32)
        ew_t = sb("ew_t", [128, 2 * UMAX, GT])
        base_r = sb("base_r", [1, 2 * UMAX])
        base_i = sb("base_i", [1, 2 * UMAX], i32)
        span = sb("span", [1, NWIN + 4])
        least = sb("least", [1, 2, len(CHUNKS) - 1])
        cuts = sb("cuts", [1, 3, REST + 1])
        cuts_i = sb("cuts_i", [1, 2, REST + 1], i32)
        cut_lo = sb("cut_lo", [1, REST + 1])
        before_i = sb("before_i", [1, 1], i32)
        acc = sb("acc", [128, KD, N + WIN])
        idx_ring = sb("idx_ring", [128, RING], i32)
        G = sb("G", [128, RING, D])
        S = sb("S", [128, RING, WIN])

        xr = sb("xr", [P, 2, CM, D])
        yr = sb("yr", [P, 2, CM, D])
        yt_sb = sb("yt_sb", [128, 2, KD, P])
        bn = sb("bn", [P, NB, 6])
        mv = sb("mv", [P, NB, 2])
        ve, sq, nwt, rstd, nmr = (sb(n, [P, NB]) for n in ("ve", "sq", "nwt", "rstd", "nmr"))
        lg, lg2, cand, oh1, oh2, mask, slotpos, prod, tot = (
            sb(n, [P, BM, X]) for n in ("lg", "lg2", "cand", "oh1", "oh2", "mask", "slotpos", "prod", "tot"))
        m1, m2, i1, i2, dl, ex = (sb(n, [P, BM]) for n in ("m1", "m2", "i1", "i2", "dl", "ex"))
        gw = sb("gw", [P, 2, BM])
        SHB, SHX = 8, 4
        scan = [sb(f"scan{k}", [P, SHB + BM, X]) for k in range(2)]
        cmp = sb("cmp", [P, X, TPE])
        tl = sb("tl", [P, X])
        scx = [sb(f"scx{k}", [P, SHX + X]) for k in range(2)]
        pos = sb("pos", [P, 2, BM])
        pos_i, hi_i, lo_i = (sb(n, [P, 2, BM], i32) for n in ("pos_i", "hi_i", "lo_i"))
        hi_f, lo_f = (sb(n, [P, 2, BM]) for n in ("hi_f", "lo_f"))
        padz = sb("padz", [128, NH])
        slot_read = [sb(f"slot_read{s.index}", [128, NHP], i32) for s in SETS]
        slot_add = [sb(f"slot_add{s.index}", [128, NHP], i32) for s in SETS]
        slot_w = [sb(f"slot_w{s.index}", [128, NHP]) for s in SETS]
        starts = [sb(f"starts{s.index}", [1, X + 1], i32) for s in SETS]

        w1_raw = sb("w1_raw", [128, KD, H])
        w2_raw = sb("w2_raw", [128, KH, D])

        def weight_parts(k):
            return [sb(f"{n}_{k}", shape, f32r) for n, shape in
                    (("w1_hi", [128, KD, H]), ("w1_lo", [128, KD, H]), ("w2_hi", [128, KH, D]), ("w2_lo", [128, KH, D]))]

        parts = [weight_parts(0)]
        with ExitStack() as early:
            x_sb = sb("x_sb", [P, NB, D], f32, early)
            xn_sb = sb("xn_sb", [P, NB, D], f32, early)
            e_int, xe_int = (sb(n, [NG, GE], i32, early) for n in ("e_int", "xe_int"))
            e_f, xe_f, we_f = (sb(n, [NG, GE], f32, early) for n in ("e_f", "xe_f", "we_f"))
            base_f = sb("base_f", [NG, 3], f32, early)
        parts.append(weight_parts(1))
        with ExitStack() as routing:
            oh_lo = sb("oh_lo", [P, 2, 2, RB, 128], f32, routing)
            oh_hi = sb("oh_hi", [P, 2, 2, RB, 2, NH], f32, routing)
        hf = sb("hf", [128, 2, 2, T])
        h_hi = sb("h_hi", [128, KH, T], f32r)
        h_lo = sb("h_lo", [128, KH, T], f32r)
        yg = sb("yg", [128, TH, D])
        y_hi = sb("y_hi", [128, KD, T], f32r)
        y_lo = sb("y_lo", [128, KD, T], f32r)
        ost = sb("ost", [128, TH, D])
        gat_i = sb("gat_i", [128, TH], i32)
        add_i = sb("add_i", [128, TH], i32)

        ps_h = pb("ps_h", [128, 2, 512])
        ps_o = pb("ps_o", [128, 2, 512])
        ps_y = pb("ps_y", [128, 512])
        ps_m = pb("ps_m", [128, 512])
        ps_agg = pb("ps_agg", [128, 2, 512])
        ps_b1 = ps_m[:, 256:256 + X * KH]
        places = (ps_m, ps_y)
        ps_gate = ps_o[0:P, 0, :]

        s_const, s_edge_zero, s_xn_rows, s_xn = sem("s_const"), sem("s_edge_zero"), sem("s_xn_rows"), sem("s_xn")
        s_dst, s_src, s_weights, s_small, s_b1 = sem("s_dst"), sem("s_src"), sem("s_weights"), sem("s_small"), sem("s_b1")
        s_x = [sem(f"s_x{c}") for c in range(NC)]
        s_dve, s_pool, s_zero_rows, s_go = sem("s_dve"), sem("s_pool"), sem("s_zero_rows"), sem("s_go")
        s_b2 = sem("s_b2")
        s_over, s_cuts = sem("s_over"), sem("s_cuts")
        s_var, s_root, s_scale = sem("s_var"), sem("s_root"), sem("s_scale")
        s_rows, s_cols, s_tables, s_b1_t, s_next = sem("s_rows"), sem("s_cols"), sem("s_tables"), sem("s_b1_t"), sem("s_next")
        s_raw1, s_raw2, s_hi1, s_hi2, s_split1, s_split2 = (
            sem(f"s_{n}") for n in ("raw1", "raw2", "hi1", "hi2", "split1", "split2"))
        pre, main = EdgeSems(sem, "pre", RING), EdgeSems(sem, "main", RING)
        ch = ChunkSems(sem, CHUNKS)
        sems = [SetSems(sem, s, TH) for s in SETS]

        block = ctx.enter_context(nc.Block())

        def split_steps(x, which):
            w1_hi, w1_lo, w2_hi, w2_lo = parts[x % 2]
            raw, hi, lo = (w1_raw, w1_hi, w1_lo) if which == 1 else (w2_raw, w2_hi, w2_lo)
            raw, hi, lo = (flat(a[:, :, :]) for a in (raw, hi, lo))
            return [(raw[:, c:c + SC], hi[:, c:c + SC], lo[:, c:c + SC]) for c in range(0, KD * H, SC)]

        BESIDE = {name: (COMPLETE[L0 - 1] + n // 2, n % 2) for n, name in enumerate(
            ("residual", "scaled", "logits", "first", "second", "scanned", "slots", "step0", "step1", "step2"))}
        assert 2 * DURING == len(BESIDE)

        def pairs_beside(c):
            return c.blocks if c.index < L0 - 1 else 1

        def steps_of(blocks):
            return [(b, min(b + RB, blocks)) for b in range(0, blocks, RB)]

        def cut_of(eng, i):
            a = eng.value_load(cuts_i[0:1, 0, i:i + 1], min_val=0, max_val=UMAX - 2)
            z = eng.value_load(cuts_i[0:1, 0, i + 1:i + 2], min_val=0, max_val=UMAX - 2)
            return a, z, eng.value_load(cuts_i[0:1, 1, i:i + 1], min_val=0, max_val=UMAX - 2)

        @block.sync
        def _(sp):
            x_v, xn_v = by_partition(x, NB), by_partition(xn_d, NB)
            for c in range(NC):
                cs = slice(c * CB, (c + 1) * CB)
                for a, z in SPANS:
                    sp.dma_start(x_sb[a:z, cs, :], x_v[a:z, cs, :]).then_inc(s_x[c], 16)
            full = (NG - 1) * GE

            def edge_rows(to, a, done, fill):
                sp.dma_start(to[0:NG - 1, :], a[0:full].rearrange("(g j) -> g j", j=GE)).then_inc(done, 16)
                sp.dma_start(to[NG - 1:NG, 0:LAST], a[full:E].rearrange("(g j) -> g j", g=1)).then_inc(done, 16)
                if fill:
                    sp.dma_start(to[NG - 1:NG, LAST:GE],
                                 a[E - (GE - LAST):E].rearrange("(g j) -> g j", g=1)).then_inc(done, 16)

            edge_rows(e_int, dst, s_dst, True)
            edge_rows(xe_int, src, s_src, True)
            sp.wait_ge(s_edge_zero, 1)
            edge_rows(we_f, edge_w, s_weights, False)
            sp.dma_start(b1_in[:, :], b1.rearrange("e (c p) -> (e c) p", p=128)).then_inc(s_b1, 16)
            for c in range(NC):
                cs = slice(c * CB, (c + 1) * CB)
                sp.wait_ge(s_xn, (c + 1) * CB)
                for a, z in SPANS:
                    sp.dma_start(xn_v[a:z, cs, :], xn_sb[a:z, cs, :]).then_inc(s_xn_rows, 16)
            sp.dma_start(bias_bc[:, :], b_gnn.partition_broadcast(128)).then_inc(s_small, 16)
            sp.dma_start(bg_bc[:, :], b_gate.partition_broadcast(128)).then_inc(s_small, 16)
            sp.dma_start(wn_sb[:, :, :], w_gnn.rearrange("(k p) n -> p k n", p=128)).then_inc(s_small, 16)
            sp.dma_start(wg_sb[:, :, :], w_gate.rearrange("(k p) n -> p k n", p=128)).then_inc(s_small, 16)
            sp.wait_ge(s_const, 1)
            sp.dma_start(out[N:N + PAD_ROWS, :].rearrange("(a p) d -> p a d", p=128), zeros[:, :, :]).then_inc(s_zero_rows, 16)

            def load_weights(x):
                if x:
                    sp.wait_ge(s_split1, STEPS * x)
                sp.dma_start(w1_raw[:, :, :], w1[x % X].rearrange("(k p) h -> p k h", p=128)).then_inc(s_raw1, 16)
                if x:
                    sp.wait_ge(s_split2, STEPS * x)
                else:
                    sp.wait_ge(main.acc, 2 * 2 + 2)
                sp.dma_start(w2_raw[:, :, :], w2[x % X].rearrange("(k p) d -> p k d", p=128)).then_inc(s_raw2, 16)

            def load_x(c):
                for a, z in SPANS:
                    sp.dma_start(xr[a:z, c.index % 2, 0:c.blocks, :], of_chunk(x, c)[a:z, :, :]).then_inc(ch.x[c.index], 16)

            load_x(CHUNKS[0])
            sp.wait_ge(main.acc, 2 + 2)
            load_weights(0)
            load_x(CHUNKS[1])
            sp.wait_ge(main.acc, 4 * 2 + 2)
            sp.dma_start(b2_bc[:, :, :], b2.partition_broadcast(128)).then_inc(s_b2, 16)
            load_weights(1)
            for s in SETS:
                first = s.chunks[0].first
                for c in s.chunks:
                    sp.wait_ge(ch.y, c.z)
                    for a, z in SPANS:
                        rows = (slice(a, z), c.index % 2, slice(0, c.blocks), slice(None))
                        sp.dma_start(of_chunk(y_d[s.index], c, first)[a:z, :, :], yr[rows]).then_inc(ch.stored[c.index], 16)
                        sp.dma_start(of_chunk(out, c)[a:z, :, :], xr[rows]).then_inc(ch.stored[c.index], 16)
                    if c.index + 2 < len(CHUNKS):
                        sp.wait_ge(ch.stored[c.index], 64)
                        load_x(CHUNKS[c.index + 2])
                for e in range(X):
                    k = s.index * X + e + 2
                    if k < len(SETS) * X:
                        load_weights(k)
            sp.wait_ge(s_zero_rows, 16)
            for done in ch.stored:
                sp.wait_ge(done, 64)

        @block.gpsimd
        def _(pool):
            own = Order(pool, s_pool).own

            def ramp(to, pattern, base=0, step=0):
                own(pool.iota(to, pattern, base=base, channel_multiplier=step, allow_small_or_imprecise_dtypes=True))

            pool.memset(we_f[:, :], 0.0).then_inc(s_edge_zero, 1)
            own(pool.memset(ident[:, :], 0.0))
            own(pool.affine_select(out=ident[:, :], in_=ident[:, :], compare_op=ALU.not_equal, fill=1.0,
                                   base=0, pattern=[[-1, 128]], channel_multiplier=1))
            own(pool.memset(ones[:, :], 1.0))
            own(pool.affine_select(out=tri[:, :], in_=ones[:, :], compare_op=ALU.is_gt, fill=0.0,
                                   base=0, pattern=[[1, 128]], channel_multiplier=-1))
            ramp(iota_w[:, :], [[1, 128]])
            ramp(iota_x[:, :], [[1, X]])
            ramp(iota_mx[:, :], [[1, X]], base=-X)
            ramp(thr[:, :, :], [[0, X], [T, TPE]])
            ramp(thr_w[:, :], [[WIN, NWIN]])
            ramp(pad_i[:, :], [[128, TH]], base=N, step=1)
            for s in SETS:
                ramp(pad_row[s.index][:, :], [[0, NH // TH], [128, TH]], base=N + 1 - s.chunks[0].first, step=1)
                for c in s.chunks:
                    ramp(node1[s.index][:, c.a - s.first_block:c.z - s.first_block], [[1, c.blocks]],
                         base=c.first - s.chunks[0].first + 1, step=c.blocks)
                own(pool.memset(slot_read[s.index][:, :], 0))
                own(pool.memset(slot_add[s.index][:, :], 0))
                own(pool.memset(slot_w[s.index][:, :], 0.0))
            for t in (rel_t, src_t, ew_t):
                own(pool.memset(t[:, NG:2 * UMAX, :], 0))
            own(pool.memset(base_r[:, NG:2 * UMAX], 0.0))
            for c in CHUNKS[:-1]:
                own(pool.memset(chunk_end[:, c.index:c.index + 1], float(c.first + c.nodes)))
            for i in range(REST + 1):
                own(pool.memset(cut_lo[:, i:i + 1], float(i - 1)))
            for k in range(2):
                own(pool.memset(scan[k][:, 0:SHB, :], 0.0))
                own(pool.memset(scx[k][:, 0:SHX], 0.0))
            own(pool.memset(zeros[:, :, :], 0.0))
            own(pool.memset(acc[:, :, :], 0.0))
            pool.sem_inc(s_const, 1)

            def gather_pair(q, u):
                for h in range(RING // 2):
                    pool.wait_ge(q.idx, u * (RING // 2) + h + 1)
                    pool.sem_inc(s_go, 1)
                    for k in (2 * h, 2 * h + 1):
                        pool.indirect_dma_start(G[:, k, :], None, xn_d,
                                                bass.IndirectOffsetOnAxis(idx_ring[:, k:k + 1], 0)).then_inc(q.gathered[k], 16)

            pool.wait_ge(s_tables, 1)
            n_pre = pool.value_load(before_i[0:1, 0:1], min_val=0, max_val=NWIN)
            pool.wait_ge(s_xn_rows, 32 * NC)
            with pool.If(n_pre):
                with pool.Fori(0, n_pre) as ps:
                    with pool.Fori(0, NP) as i:
                        gather_pair(pre, ps * NP + i)
                pool.wait_ge(pre.acc, n_pre * NG + 2)
            with pool.Fori(0, U0 + 1) as u:
                gather_pair(main, u)

            for s, q in zip(SETS, sems):
                k = s.index
                if k == 0:
                    own(pool.memset(ost[:, :, :], 0.0))
                pool.wait_ge(s_zero_rows, 16)
                for h in range(TH):
                    pool.indirect_dma_start(out, bass.IndirectOffsetOnAxis(pad_i[:, h:h + 1], 0),
                                            zeros[:, h, :], None, compute_op=ALU.add).then_inc(q.added[h], 16)
                pool.wait_ge(q.route, 1)
                for c in s.chunks:
                    pool.wait_ge(ch.stored[c.index], 64)

                def gather(tile, n):
                    pool.tensor_copy(gat_i[:, :], slot_read[k][:, bass.ds(tile * TH, TH)]).then_inc(q.index, 1)
                    pool.wait_ge(q.index, n)
                    pool.sem_inc(s_go, 1)
                    for h in range(TH):
                        pool.indirect_dma_start(yg[:, h, :], None, y_d[k],
                                                bass.IndirectOffsetOnAxis(gat_i[:, h:h + 1], 0)).then_inc(q.tile_in[h], 16)

                gather(0, 1)
                pool.wait_ge(q.tile_t, 1)
                gather(1, 2)
                for e in range(X):
                    first = pool.value_load(starts[k][0:1, e:e + 1], min_val=e, max_val=s.max_tiles - 1)
                    end = pool.value_load(starts[k][0:1, e + 1:e + 2], min_val=e + 1, max_val=s.max_tiles)
                    nxt = k * X + e + 1
                    if k == 1 and nxt < len(SETS) * X:
                        for n, (raw, hi, lo) in enumerate(split_steps(nxt, 1)):
                            pool.wait_ge(s_hi1, STEPS * nxt + n + 1)
                            pool.tensor_tensor(lo, raw, hi.bitcast(f32), ALU.subtract).then_inc(s_split1, 1)
                    with pool.Fori(first, end) as g:
                        pool.wait_ge(q.tile_t, g + 2)
                        gather(g + 2, g * 2 + 3)
                        if k == 0:
                            gather_pair(main, g + (U0 + 1))
                        for h in range(TH):
                            pool.wait_ge(q.added[h], (g + 1) * 16)
                        pool.tensor_copy(add_i[:, :], slot_add[k][:, bass.ds(g * TH, TH)]).then_inc(q.index, 1)
                        pool.wait_ge(q.index, g * 2 + 4)
                        pool.wait_ge(q.staged, (g + 1) * TH)
                        pool.sem_inc(s_go, 1)
                        for h in range(TH):
                            pool.indirect_dma_start(out, bass.IndirectOffsetOnAxis(add_i[:, h:h + 1], 0),
                                                    ost[:, h, :], None, compute_op=ALU.add).then_inc(q.added[h], 16)
                for h in range(TH):
                    pool.wait_ge(q.added[h], (end + 1) * 16)
                    pool.wait_ge(q.tile_in[h], (end + 2) * 16)
                if k == 0:
                    pool.sem_inc(s_go, 1)
                    pool.wait_ge(s_cuts, 1)
                    n = pool.value_load(cuts_i[0:1, 1, REST:REST + 1], min_val=0, max_val=NP - 1)
                    with pool.If(n):
                        with pool.Fori(end + (U0 + 1), NP) as u:
                            gather_pair(main, u)

        @block.scalar
        def _(act):
            def root(var, done, waited, a, z):
                act.wait_ge(var, waited)
                nc.scalar.activation(sq[:, a:z], ve[:, a:z], ACT.Sqrt).then_inc(done, 1)

            for c in range(NC + 1):
                if c < NC:
                    root(s_var, s_root, c + 1, c * CB, (c + 1) * CB)
                if c >= 1:
                    act.wait_ge(s_scale, c)
                    for b in range((c - 1) * CB, c * CB):
                        nc.scalar.activation(xn_sb[:, b, :], x_sb[:, b, :], ACT.Identity, bias=nmr[:, b:b + 1],
                                             scale=rstd[:, b:b + 1]).then_inc(s_xn, 1)

            src_v = flat(src_t[:, :, :])

            def numbers(q, u, i, j):
                for h in (2 * j, 2 * j + 1):
                    act.wait_ge(q.used, u * RING + 2 * h + 2)
                    nc.scalar.activation(idx_ring[:, 2 * h:2 * h + 2],
                                         src_v[:, bass.ds(i * RING + 2 * h, 2)], ACT.Copy).then_inc(q.idx, 1)

            def split_high(x, which, steps=range(STEPS)):
                raw_in, done = ((s_raw1, s_hi1), (s_raw2, s_hi2))[which - 1]
                act.wait_ge(raw_in, 16 * (x + 1))
                for n in steps:
                    raw, hi, lo = split_steps(x, which)[n]
                    nc.scalar.activation(hi, raw, ACT.Copy).then_inc(done, 1)

            act.wait_ge(s_tables, 1)
            n_pre = act.value_load(before_i[0:1, 0:1], min_val=0, max_val=NWIN)
            with act.If(n_pre):
                with act.Fori(0, n_pre) as ps:
                    with act.Fori(0, NP) as i:
                        for j in range(2):
                            numbers(pre, ps * NP + i, i, j)
                act.wait_ge(pre.acc, n_pre * NG + 2)
                act.sem_inc(s_over, 1)
            for j in range(2):
                numbers(main, 0, 0, j)

            def group(u, j):
                numbers(main, u + 1, u + 1, j)

            def pair(u):
                group(u, 0)
                group(u, 1)

            def groups_from(u):
                left = iter([(v, j) for v in range(u, u + CM) for j in range(2)])
                return lambda: group(*next(left))

            def pairs(a, z):
                with act.Fori(a, z) as u:
                    pair(u)

            def normalise(c):
                act.wait_ge(ch.scale, c.index + 1)
                if c.index >= 2:
                    act.wait_ge(ch.stored[c.index - 2], 64)
                for b in range(c.a, c.z):
                    place = (slice(None), c.index % 2, b - c.a, slice(None))
                    nc.scalar.activation(yr[place], xr[place], ACT.Identity, bias=nmr[:, b:b + 1],
                                         scale=rstd[:, b:b + 1]).then_inc(ch.y, 1)

            def copy_turned(c, beside=lambda: None):
                for b in range(c.a, c.z):
                    if b > c.a:
                        beside()
                    act.wait_ge(ch.yt, b + 1)
                    if b >= 2:
                        act.wait_ge(ch.gate, b - 1)
                    nc.scalar.activation(yt_sb[:, b % 2, :, :],
                                         places[b % 2][:, 0:KD * 128].rearrange("q (k p) -> q k p", p=128)[:, :, 0:P],
                                         ACT.Copy).then_inc(ch.yt_sb, 1)

            def chunk_root(c):
                root(ch.var, ch.root, c.index + 1, c.a, c.z)

            done = 0
            for which in (1, 2):
                for n in range(STEPS):
                    u = COMPLETE[0] - 2 * STEPS + (which - 1) * STEPS + n
                    pairs(done, u)
                    split_high(0, which, [n])
                    done = u
            for c in SETS[0].chunks:
                u = COMPLETE[c.index]
                pairs(done, u)
                if c.index < L0 - 1:
                    beside = groups_from(u)
                    for b in range(c.a, c.z - 1):
                        beside()
                    chunk_root(c)
                    beside()
                    normalise(c)
                    beside()
                    copy_turned(c, beside)
                else:
                    chunk_root(c)
                    group(u, 0)
                    normalise(c)
                    group(u, 1)
                    copy_turned(c)
                done = u + pairs_beside(c)

            for s, q in zip(SETS, sems):
                k = s.index

                def aside(name):
                    if k == 0:
                        group(*BESIDE[name])

                if k == 1:
                    def rest(i, j=None):
                        a, z, n = cut_of(act, i)
                        with act.If(n):
                            if j is None:
                                pairs(a, z)
                            else:
                                group(a, j)

                    c0, c1, c2 = s.chunks
                    act.wait_ge(s_cuts, 1)
                    rest(0)
                    chunk_root(c0)
                    rest(1, 0)
                    normalise(c0)
                    rest(1, 1)
                    chunk_root(c1)
                    rest(2, 0)
                    copy_turned(c0)
                    normalise(c1)
                    rest(2, 1)
                    rest(3, 0)
                    copy_turned(c1)
                    rest(3, 1)
                    rest(4)
                    rest(5)
                    chunk_root(c2)
                    normalise(c2)
                    copy_turned(c2)
                aside("logits")
                aside("first")
                act.wait_ge(q.delta, 1)
                nc.scalar.activation(ex[:, 0:s.blocks], dl[:, 0:s.blocks], ACT.Exp).then_inc(q.exp, 1)
                for name in ("second", "scanned", "slots", "step0", "step1", "step2"):
                    aside(name)

                act.wait_ge(q.route, 1)
                act.wait_ge(s_b1_t, 1)
                for e in range(X):
                    nxt = k * X + e + 1
                    first = act.value_load(starts[k][0:1, e:e + 1], min_val=e, max_val=s.max_tiles - 1)
                    end = act.value_load(starts[k][0:1, e + 1:e + 2], min_val=e + 1, max_val=s.max_tiles)
                    if k * X + e == 0:
                        split_high(1, 1)
                    with act.Fori(first, end) as g:
                        for j in range(NQ):
                            act.wait_ge(q.hidden, g * NQ + j + 1)
                            act.wait_ge(q.h_split, g * NQ + j + 1)
                            for m in range(2):
                                c = 2 * j + m
                                nc.scalar.activation(hf[:, j % 2, m, :], ps_h[:, j % 2, m * T:(m + 1) * T], ACT.Gelu,
                                                     bias=b1_t[:, e * KH + c:e * KH + c + 1]).then_inc(q.gelu, 1)
                        if k == 0:
                            pair(g + U0)
                    if nxt < len(SETS) * X:
                        if e >= 1:
                            act.wait_ge(q.result, first)
                        split_high(nxt, 2)
                    if nxt + 1 < len(SETS) * X:
                        act.wait_ge(q.hidden, end * NQ)
                        split_high(nxt + 1, 1)

        @block.tensor
        def _(pe):
            pe.wait_ge(s_const, 1)
            banks = (ps_h[:, 0, :], ps_h[:, 1, :], ps_y[:, :])
            for k, rows in enumerate((e_f, xe_f, we_f)):
                if k < 2:
                    pe.wait_ge(s_rows, k + 1)
                else:
                    pe.wait_ge(s_weights, 32)
                for c in range(GT):
                    last = nc.tensor.transpose(banks[k][:, c * NG:(c + 1) * NG], rows[:, c * 128:(c + 1) * 128],
                                               ident[0:NG, 0:NG])
                last.then_inc(s_cols, 1)
            for k in range(2):
                nc.tensor.transpose(ps_m[0:1, k * 128:k * 128 + NG], base_f[:, 2 * k:2 * k + 1], ident[0:NG, 0:NG])
            pe.wait_ge(s_b1, 16)
            nc.tensor.transpose(ps_b1, b1_in[:, :], ident[0:X * KH, 0:X * KH]).then_inc(s_cols, 1)

            def sum_group(q, u, j):
                pe.wait_ge(q.acc, u * 2 + j + 1)
                for c in range(GT):
                    k = j * GT + c
                    pe.wait_ge(q.window, u * RING + k + 1)
                    pe.wait_ge(q.gathered[k], (u + 1) * 16)
                    for m in range(KD):
                        last = nc.tensor.matmul(ps_agg[:, j, m * WIN:(m + 1) * WIN],
                                                G[:, k, m * 128:(m + 1) * 128], S[:, k, :],
                                                start=(c == 0 and m == 0), stop=(c == GT - 1 and m == KD - 1))
                    last.then_inc(q.used, 1)

            pe.wait_ge(s_tables, 1)
            n_pre = pe.value_load(before_i[0:1, 0:1], min_val=0, max_val=NWIN)
            pe.sem_inc(pre.used, RING)
            pe.sem_inc(main.used, RING)
            with pe.If(n_pre):
                with pe.Fori(0, n_pre) as ps:
                    with pe.Fori(0, NP) as i:
                        for j in range(2):
                            sum_group(pre, ps * NP + i, j)
                pe.wait_ge(pre.acc, n_pre * NG + 2)

            def group(u, j):
                sum_group(main, u, j)

            def pair(u):
                group(u, 0)
                group(u, 1)

            def groups_from(u):
                left = iter([(v, j) for v in range(u, u + CM) for j in range(2)])
                return lambda: group(*next(left))

            def pairs(a, z):
                with pe.Fori(a, z) as u:
                    pair(u)

            free = [None, None]

            def take_place(b, read):
                if free[b % 2]:
                    pe.wait_ge(*free[b % 2])
                free[b % 2] = (read, b + 1)

            def linear(c, a, z):
                pe.wait_ge(main.acc, COMPLETE[c.index] * 2 + 2)
                v = acc[:, :, c.first:c.first + c.nodes].rearrange("q k (p b) -> q k b p", b=c.blocks)
                for b in range(a, z):
                    take_place(b, ch.sum)
                    for m in range(KD):
                        last = nc.tensor.matmul(places[b % 2][0:P, 0:D], v[:, m, b - c.a, :], wn_sb[:, m, :],
                                                start=(m == 0), stop=(m == KD - 1))
                    last.then_inc(ch.lin, 1)

            def gate(c, b):
                pe.wait_ge(ch.yt_sb, b + 1)
                if c.index and b == c.a:
                    pe.wait_ge(ch.logits, c.index)
                for m in range(KD):
                    last = nc.tensor.matmul(ps_gate[:, (b - c.a) * X:(b - c.a + 1) * X], yt_sb[:, b % 2, m, :],
                                            wg_sb[:, m, :], start=(m == 0), stop=(m == KD - 1))
                last.then_inc(ch.gate, 1)

            def turn(c, a, z):
                for b in range(a, z):
                    pe.wait_ge(ch.y, b + 1)
                    take_place(b, ch.yt_sb)
                    for m in range(KD):
                        last = nc.tensor.transpose(places[b % 2][:, m * 128:m * 128 + P],
                                                   yr[:, c.index % 2, b - c.a, m * 128:(m + 1) * 128], ident[0:P, 0:P])
                    last.then_inc(ch.yt, 1)
                    if b > c.a:
                        gate(c, b - 1)
                if z == c.z:
                    gate(c, z - 1)

            done = 0
            for c in SETS[0].chunks:
                u = COMPLETE[c.index]
                pairs(done, u)
                if c.index == 0:
                    pe.wait_ge(s_small, 16 * 4)
                if c.index < L0 - 1:
                    beside = groups_from(u)
                    for b in range(c.a, c.z):
                        linear(c, b, b + 1)
                        beside()
                    beside()
                    for b in range(c.a, c.z):
                        turn(c, b, b + 1)
                        if b + 1 < c.z:
                            beside()
                else:
                    linear(c, c.a, c.z)
                    group(u, 0)
                    group(u, 1)
                    turn(c, c.a, c.z)
                done = u + pairs_beside(c)

            for s, q in zip(SETS, sems):
                k, B = s.index, s.blocks

                def aside(name):
                    if k == 0:
                        group(*BESIDE[name])

                if k == 1:
                    def rest(i, j=None):
                        a, z, n = cut_of(pe, i)
                        with pe.If(n):
                            if j is None:
                                pairs(a, z)
                            else:
                                group(a, j)

                    c0, c1, c2 = s.chunks
                    pe.wait_ge(sems[0].biased, end + 1)
                    pe.wait_ge(sems[0].y_split, end + 1)
                    pe.sem_inc(s_over, 1)
                    pe.wait_ge(s_cuts, 1)
                    rest(0)
                    linear(c0, c0.a, c0.z)
                    rest(1, 0)
                    rest(1, 1)
                    linear(c1, c1.a, c1.z)
                    rest(2, 0)
                    turn(c0, c0.a, c0.z)
                    rest(2, 1)
                    rest(3, 0)
                    turn(c1, c1.a, c1.z)
                    rest(3, 1)
                    rest(4)
                    rest(5)
                    linear(c2, c2.a, c2.z)
                    turn(c2, c2.a, c2.z)

                for name in ("logits", "first", "second"):
                    aside(name)
                pe.wait_ge(q.mask, 1)
                mk = flat(mask[:, 0:B, :])
                nc.tensor.matmul(ps_o[0:P, 0, 0:B * X], tri[0:P, 0:P], mk, start=True, stop=True)
                nc.tensor.matmul(ps_o[0:P, 1, 0:B * X], ones[0:P, 0:P], mk, start=True, stop=True).then_inc(q.rank, 1)
                for name in ("scanned", "slots"):
                    aside(name)
                ps_inv = ps_m[:, 0:2 * NH]
                for n, (lo, hi) in enumerate(steps_of(B)):
                    if n < 3:
                        aside(f"step{n}")
                    pe.wait_ge(q.onehot, 3 * n + 3)
                    for j in range(2):
                        for b in range(hi - lo):
                            last = nc.tensor.matmul(ps_inv, oh_lo[:, n % 2, j, b, :],
                                                    oh_hi[:, n % 2, j, b, :, :].rearrange("p a h -> p (a h)"),
                                                    start=(n == 0 and j == 0 and b == 0),
                                                    stop=(hi == B and j == 1 and b == hi - lo - 1))
                    last.then_inc(q.onehot_used, 1)

                def transpose_tile(n):
                    for h in range(TH):
                        pe.wait_ge(q.tile_in[h], n * 16)
                    for h in range(TH):
                        for m in range(KD):
                            last = nc.tensor.transpose(ps_y[:, m * T + h * 128:m * T + (h + 1) * 128],
                                                       yg[:, h, m * 128:(m + 1) * 128], ident[:, :])
                    last.then_inc(q.tile_t, 1)

                pe.wait_ge(q.route, 1)
                transpose_tile(1)
                pe.sem_inc(q.biased, 1)
                pe.sem_inc(q.gelu, 4)
                pe.sem_inc(q.h_split, 2)
                for e in range(X):
                    cur = k * X + e
                    w1_hi, w1_lo, w2_hi, w2_lo = parts[cur % 2]
                    first = pe.value_load(starts[k][0:1, e:e + 1], min_val=e, max_val=s.max_tiles - 1)
                    end = pe.value_load(starts[k][0:1, e + 1:e + 2], min_val=e + 1, max_val=s.max_tiles)
                    pe.wait_ge(s_split1, STEPS * (cur + 1))
                    with pe.Fori(first, end) as g:
                        pe.wait_ge(q.y_split, g + 1)
                        for j in range(NQ):
                            pe.wait_ge(q.gelu, (g * NQ + j) * 2 + 2)
                            for m2_ in range(2):
                                c = 2 * j + m2_
                                terms = [(m, a, b) for m in range(KD) for a, b in
                                         ((w1_hi, y_hi), (w1_hi, y_lo), (w1_lo, y_hi))]
                                for n, (m, a, b) in enumerate(terms):
                                    last = nc.tensor.matmul(ps_h[:, j % 2, m2_ * T:(m2_ + 1) * T],
                                                            a[:, m, c * 128:(c + 1) * 128], b[:, m, :],
                                                            start=(n == 0), stop=(n == len(terms) - 1))
                            last.then_inc(q.hidden, 1)
                        transpose_tile(g + 2)
                        if k == 0:
                            pair(g + U0)
                        pe.wait_ge(q.biased, g + 1)
                        pe.wait_ge(s_split2, STEPS * (cur + 1))
                        for j in range(NQ):
                            pe.wait_ge(q.h_split, g * NQ + j + 3)
                            for c in (2 * j, 2 * j + 1):
                                for n, (a, b) in enumerate(((h_hi, w2_hi), (h_hi, w2_lo), (h_lo, w2_hi))):
                                    for h in range(TH):
                                        last = nc.tensor.matmul(ps_o[:, h, 0:D], a[:, c, h * 128:(h + 1) * 128],
                                                                b[:, c, :], start=(c == 0 and n == 0),
                                                                stop=(c == KH - 1 and n == 2))
                        last.then_inc(q.result, 1)

        @block.vector
        def _(dve):
            order = Order(dve, s_dve)
            own, mark, need = order.own, order.mark, order.need
            V = nc.vector

            def stats(a, z):
                seen = []
                for b in range(a, z + 1):
                    if b < z:
                        seen.append(mark(V.bn_stats(bn[:, b, :], x_sb[:, b, :])))
                    if b > a:
                        need(seen[b - 1 - a])
                        last = mark(V.bn_aggr(mv[:, b - 1, :], bn[:, b - 1, :]))
                need(last)
                V.tensor_scalar(ve[:, a:z], mv[:, a:z, 1], EPS, 0.25, ALU.add, ALU.mult).then_inc(s_var, 1)

            def scales(roots, done, waited, a, z):
                dve.wait_ge(roots, waited)
                own(V.reciprocal(nwt[:, a:z], sq[:, a:z]))
                own(V.tensor_tensor(nwt[:, a:z], nwt[:, a:z], ve[:, a:z], ALU.mult))
                own(V.tensor_tensor(nwt[:, a:z], nwt[:, a:z], sq[:, a:z], ALU.add))
                own(V.reciprocal(rstd[:, a:z], nwt[:, a:z]))
                V.scalar_tensor_tensor(out=nmr[:, a:z], in0=mv[:, a:z, 0], scalar=-1.0, in1=rstd[:, a:z],
                                       op0=ALU.mult, op1=ALU.mult).then_inc(done, 1)

            for c in range(NC + 1):
                if c < NC:
                    dve.wait_ge(s_x[c], 32)
                    stats(c * CB, (c + 1) * CB)
                if c >= 1:
                    scales(s_root, s_scale, c, (c - 1) * CB, c * CB)

            dve.wait_ge(s_dst, 48)
            own(V.tensor_copy(e_f[:, :], e_int[:, :]))
            own(V.tensor_reduce(base_f[:, 0:1], e_f[:, :], AX.X, ALU.min))
            n_max = mark(V.tensor_reduce(base_f[:, 1:2], e_f[:, :], AX.X, ALU.max))
            dve.wait_ge(s_src, 48)
            V.tensor_copy(xe_f[:, :], xe_int[:, :])
            need(n_max)
            own(V.tensor_tensor(base_f[:, 2:3], base_f[:, 1:2], base_f[:, 0:1], ALU.subtract))
            own(V.tensor_scalar(e_f[:, :], e_f[:, :], base_f[:, 0:1], None, ALU.subtract))
            dve.sem_inc(s_rows, 2)
            dve.wait_ge(s_const, 1)
            banks = (ps_h[:, 0, :], ps_h[:, 1, :], ps_y[:, :])
            for k, to in enumerate((rel_t, src_t, ew_t)):
                dve.wait_ge(s_cols, k + 1)
                V.tensor_copy(to[:, 0:NG, :], banks[k][:, 0:GT * NG].rearrange("p (c g) -> p g c", g=NG))
            dve.wait_ge(s_cols, 4)
            own(V.tensor_copy(base_r[:, 0:NG], ps_m[0:1, 0:NG]))
            V.tensor_copy(b1_t[:, :], ps_b1).then_inc(s_b1_t, 1)
            own(V.tensor_reduce(span[:, 0:1], ps_m[0:1, 128:128 + NG], AX.X, ALU.max))
            V.tensor_copy(base_i[:, :], base_r[:, :])
            own(V.tensor_scalar(span[:, 4:4 + NWIN], thr_w[:, :], span[:, 0:1], None, ALU.is_le))
            own(V.tensor_reduce(span[:, 1:2], span[:, 4:4 + NWIN], AX.X, ALU.add))
            for c in CHUNKS[:-1]:
                n = mark(V.tensor_reduce(least[:, 0, c.index:c.index + 1], base_r[:, 2 * COMPLETE[c.index]:NG], AX.X, ALU.min))
            need(n)
            own(V.tensor_tensor(least[:, 1, :], least[:, 0, :], chunk_end[:, :], ALU.is_lt))
            own(V.tensor_reduce(span[:, 2:3], least[:, 1, :], AX.X, ALU.max))
            own(V.tensor_scalar(span[:, 3:4], span[:, 1:2], 1.0, None, ALU.is_gt))
            own(V.tensor_tensor(span[:, 2:3], span[:, 2:3], span[:, 3:4], ALU.max))
            own(V.tensor_tensor(span[:, 2:3], span[:, 2:3], span[:, 1:2], ALU.mult))
            own(V.tensor_copy(before_i[:, :], span[:, 2:3]))
            dve.sem_inc(s_tables, 1)

            rel_v, ew_v = flat(rel_t[:, :, :]), flat(ew_t[:, :, :])

            def windows(q, u, i, j):
                dve.wait_ge(q.used, u * RING + (j + 1) * GT)
                for k in range(j * GT, (j + 1) * GT):
                    t = bass.ds(i * RING + k, 1)
                    V.tensor_scalar(S[:, k, :], iota_w[:, 0:WIN], rel_v[:, t], ew_v[:, t],
                                    ALU.is_equal, ALU.mult).then_inc(q.window, 1)

            def add_group(q, u, i, j):
                base = dve.value_load(base_i[0:1, bass.ds(i * 2 + j, 1)], min_val=0, max_val=N)
                dve.wait_ge(q.used, (u + 1) * RING + (j + 1) * GT)
                dve.wait_ge(q.acc, u * 2 + j + 2)
                to = acc[:, :, bass.ds(base, WIN)]
                V.tensor_tensor(to, to, ps_agg[:, j, 0:KD * WIN].rearrange("q (k w) -> q k w", k=KD),
                                ALU.add).then_inc(q.acc, 1)

            def split_low(x, which, steps=range(STEPS)):
                high, done = ((s_hi1, s_split1), (s_hi2, s_split2))[which - 1]
                for n in steps:
                    raw, hi, lo = split_steps(x, which)[n]
                    dve.wait_ge(high, STEPS * x + n + 1)
                    V.tensor_tensor(lo, raw, hi.bitcast(f32), ALU.subtract).then_inc(done, 1)

            dve.sem_inc(pre.acc, 2)
            dve.sem_inc(main.acc, 2)
            n_pre = dve.value_load(before_i[0:1, 0:1], min_val=0, max_val=NWIN)
            with dve.If(n_pre):
                with dve.Fori(0, n_pre) as ps:
                    with dve.Fori(0, NP) as i:
                        for j in range(2):
                            windows(pre, ps * NP + i, i, j)
                        for j in range(2):
                            add_group(pre, ps * NP + i, i, j)
                    V.tensor_scalar(rel_v, rel_v, float(-WIN), None, ALU.add).then_inc(s_next, 1)
                    V.tensor_scalar(base_r[:, :], base_r[:, :], float(WIN), float(N), ALU.add, ALU.min).then_inc(s_next, 1)
                    dve.wait_ge(s_next, ps * 3 + 2)
                    V.tensor_copy(base_i[:, :], base_r[:, :]).then_inc(s_next, 1)
                    dve.wait_ge(s_next, ps * 3 + 3)
                dve.wait_ge(pre.acc, n_pre * NG + 2)
                V.memset(ew_v, 0.0).then_inc(s_next, 1)
                dve.wait_ge(s_next, n_pre * 3 + 1)
                dve.sem_inc(s_over, 1)
            for j in range(2):
                windows(main, 0, 0, j)

            def group(u, j):
                add_group(main, u, u, j)
                windows(main, u + 1, u + 1, j)

            def pair(u):
                group(u, 0)
                group(u, 1)

            def groups_from(u):
                left = iter([(v, j) for v in range(u, u + CM) for j in range(2)])
                return lambda: group(*next(left))

            def pairs(a, z):
                with dve.Fori(a, z) as u:
                    pair(u)

            def bias(c):
                dve.wait_ge(ch.x[c.index], 32)
                place = xr[:, c.index % 2, 0:c.blocks, :]
                own(V.tensor_tensor(place, place, bias_bc[0:P, :].unsqueeze(1).to_broadcast([P, c.blocks, D]), ALU.add))

            def residual(c, beside=lambda: None):
                seen = []
                for b in range(c.a, c.z + 2):
                    if b < c.z:
                        dve.wait_ge(ch.lin, b + 1)
                        place = xr[:, c.index % 2, b - c.a, :]
                        V.tensor_tensor(place, places[b % 2][0:P, 0:D], place, ALU.add).then_inc(ch.sum, 1)
                    if c.a < b <= c.z:
                        dve.wait_ge(ch.sum, b)
                        seen.append(mark(V.bn_stats(bn[:, b - 1, :], xr[:, c.index % 2, b - 1 - c.a, :])))
                    if b >= c.a + 2:
                        need(seen[b - 2 - c.a])
                        last = mark(V.bn_aggr(mv[:, b - 2, :], bn[:, b - 2, :]))
                    if b < c.z - 1:
                        beside()
                need(last)
                V.tensor_scalar(ve[:, c.a:c.z], mv[:, c.a:c.z, 1], EPS, 0.25, ALU.add, ALU.mult).then_inc(ch.var, 1)

            def chunk_scales(c):
                scales(ch.root, ch.scale, c.index + 1, c.a, c.z)

            def logits(c):
                dve.wait_ge(ch.gate, c.z)
                b0 = SETS[c.index >= L0].first_block
                V.tensor_tensor(lg[:, c.a - b0:c.z - b0, :],
                                ps_gate[:, 0:c.blocks * X].rearrange("p (b e) -> p b e", e=X),
                                bg_bc[0:P, :].unsqueeze(1).to_broadcast([P, c.blocks, X]), ALU.add).then_inc(ch.logits, 1)

            done = 0
            for which in (1, 2):
                for n in range(STEPS):
                    u = COMPLETE[0] - 2 * STEPS + (which - 1) * STEPS + n
                    pairs(done, u)
                    split_low(0, which, [n])
                    done = u
            for c in SETS[0].chunks:
                u = COMPLETE[c.index]
                pairs(done, u)
                if c.index == 0:
                    dve.wait_ge(s_small, 16 * 4)
                    bias(c)
                if c.index < L0 - 1:
                    beside = groups_from(u)
                    residual(c, beside)
                    beside()
                    chunk_scales(c)
                    for b in range(c.a, c.z):
                        beside()
                else:
                    residual(c)
                    group(u, 0)
                    chunk_scales(c)
                    group(u, 1)
                logits(c)
                if c.index + 1 < L0:
                    bias(CHUNKS[c.index + 1])
                done = u + pairs_beside(c)

            for s, q in zip(SETS, sems):
                k, B = s.index, s.blocks

                def aside(name):
                    if k == 0:
                        group(*BESIDE[name])

                if k == 1:
                    def rest(i, j=None):
                        a, z, n = cut_of(dve, i)
                        with dve.If(n):
                            if j is None:
                                pairs(a, z)
                            else:
                                group(a, j)

                    own(V.tensor_scalar(cuts[:, 2, 0:1], starts[0][:, X:X + 1], float(U0), None, ALU.add))
                    own(V.tensor_scalar(cuts[:, 2, 1:2], cuts[:, 2, 0:1], float(NP - REST + 1), None, ALU.max))
                    own(V.tensor_scalar(cuts[:, 2, 2:3], cuts[:, 2, 0:1], float(NP), None, ALU.max))
                    own(V.tensor_scalar(cuts[:, 0, :], cut_lo[:, :], cuts[:, 2, 1:2], cuts[:, 2, 2:3], ALU.add, ALU.min))
                    own(V.tensor_copy(cuts[:, 0, 0:1], cuts[:, 2, 0:1]))
                    own(V.tensor_tensor(cuts[:, 1, 0:REST], cuts[:, 0, 1:REST + 1], cuts[:, 0, 0:REST], ALU.subtract))
                    own(V.tensor_scalar(cuts[:, 1, REST:REST + 1], cuts[:, 2, 0:1], -1.0, float(NP - 1), ALU.mult, ALU.add))
                    own(V.tensor_scalar(cuts[:, 1, REST:REST + 1], cuts[:, 1, REST:REST + 1], 0.0, None, ALU.max))
                    own(V.tensor_copy(cuts_i[:, :, :], cuts[:, 0:2, :]))
                    dve.sem_inc(s_cuts, 1)
                    c0, c1, c2 = s.chunks
                    bias(c0)
                    rest(0)
                    residual(c0)
                    bias(c1)
                    rest(1, 0)
                    chunk_scales(c0)
                    rest(1, 1)
                    residual(c1)
                    chunk_scales(c1)
                    rest(2, 0)
                    logits(c0)
                    rest(2, 1)
                    rest(3, 0)
                    logits(c1)
                    bias(c2)
                    rest(3, 1)
                    rest(4)
                    rest(5)
                    residual(c2)
                    chunk_scales(c2)
                    logits(c2)
                dve.wait_ge(ch.logits, s.chunks[-1].index + 1)

                def cut(a):
                    return a[:, 0:B, :] if len(a.shape) == 3 else a[:, 0:B]

                def bc(a):
                    return a.unsqueeze(2).to_broadcast([P, B, X])

                def bx(a):
                    return a.unsqueeze(1).to_broadcast([P, B, X])

                def per_block(a):
                    return a.rearrange("p (b e) -> p b e", e=X)

                def choose(logit, m, i, oh):
                    own(V.tensor_reduce(cut(m), cut(logit), AX.X, ALU.max))
                    own(V.tensor_tensor(cut(cand), cut(logit), bc(cut(m)), ALU.is_equal))
                    own(V.scalar_tensor_tensor(out=cut(cand), in0=cut(cand), scalar=float(-X), in1=bx(iota_x[0:P, :]),
                                               op0=ALU.mult, op1=ALU.add))
                    own(V.tensor_reduce(cut(i), cut(cand), AX.X, ALU.min))
                    own(V.tensor_tensor(cut(oh), bx(iota_mx[0:P, :]), bc(cut(i)), ALU.is_equal))

                aside("logits")
                choose(lg, m1, i1, oh1)
                aside("first")
                own(V.scalar_tensor_tensor(out=cut(lg2), in0=cut(oh1), scalar=NEG, in1=cut(lg), op0=ALU.mult, op1=ALU.add))
                choose(lg2, m2, i2, oh2)
                V.tensor_tensor(cut(mask), cut(oh1), cut(oh2), ALU.add).then_inc(q.mask, 1)
                V.tensor_tensor(cut(dl), cut(m2), cut(m1), ALU.subtract).then_inc(q.delta, 1)
                aside("second")

                dve.wait_ge(q.rank, 1)
                ps_rank, ps_tot = per_block(ps_o[0:P, 0, 0:B * X]), per_block(ps_o[0:P, 1, 0:B * X])
                V.tensor_copy(cut(tot), ps_tot)
                own(V.tensor_copy(scan[0][:, SHB:SHB + B, :], ps_tot))
                cur, step = 0, 1
                while step < B:
                    a, b = scan[cur], scan[1 - cur]
                    own(V.tensor_tensor(b[:, SHB:SHB + B, :], a[:, SHB:SHB + B, :], a[:, SHB - step:SHB + B - step, :], ALU.add))
                    cur, step = 1 - cur, step * 2
                run = scan[cur]
                dve.wait_ge(q.exp, 1)
                mark(V.tensor_scalar(cut(dl), cut(ex), 1.0, None, ALU.add))
                chosen = run[:, SHB + B - 1, :]
                own(V.tensor_tensor(cmp[:, :, :], thr[0:P, :, :], chosen.unsqueeze(2).to_broadcast([P, X, TPE]), ALU.is_lt))
                mark(V.reciprocal(gw[:, 0, 0:B], cut(dl)))
                own(V.tensor_reduce(tl[:, :], cmp[:, :, :], AX.X, ALU.add))
                V.tensor_tensor(gw[:, 1, 0:B], cut(ex), gw[:, 0, 0:B], ALU.mult)
                own(V.tensor_scalar(scx[0][:, SHX:SHX + X], tl[:, :], 1.0, None, ALU.max))
                own(V.tensor_tensor(cut(slotpos), run[:, SHB:SHB + B, :], cut(tot), ALU.subtract))
                cx, step = 0, 1
                while step < X:
                    a, b = scx[cx], scx[1 - cx]
                    own(V.tensor_tensor(b[:, SHX:SHX + X], a[:, SHX:SHX + X], a[:, SHX - step:SHX + X - step], ALU.add))
                    cx, step = 1 - cx, step * 2
                before = scx[cx][:, SHX - 1:SHX + X - 1]
                V.tensor_copy(starts[k][:, :], scx[cx][0:1, SHX - 1:SHX + X])
                aside("scanned")
                own(V.tensor_tensor(cut(slotpos), cut(slotpos), ps_rank, ALU.add))
                own(V.scalar_tensor_tensor(out=cut(slotpos), in0=bx(before), scalar=float(T), in1=cut(slotpos),
                                           op0=ALU.mult, op1=ALU.add))
                own(V.tensor_tensor(cut(prod), cut(oh1), cut(slotpos), ALU.mult))
                n_p = mark(V.tensor_tensor(cut(cand), cut(oh2), cut(slotpos), ALU.mult))
                V.tensor_reduce(pos[:, 0, 0:B], cut(prod), AX.X, ALU.add)
                need(n_p)
                own(V.tensor_reduce(pos[:, 1, 0:B], cut(cand), AX.X, ALU.add))
                own(V.tensor_copy(pos_i[:, :, 0:B], pos[:, :, 0:B]))
                V.tensor_scalar(hi_i[:, :, 0:B], pos_i[:, :, 0:B], 7, None, ALU.arith_shift_right)
                own(V.tensor_scalar(lo_i[:, :, 0:B], pos_i[:, :, 0:B], 127, None, ALU.bitwise_and))
                V.tensor_copy(hi_f[:, :, 0:B], hi_i[:, :, 0:B])
                own(V.tensor_copy(lo_f[:, :, 0:B], lo_i[:, :, 0:B]))
                aside("slots")
                for n, (lo, hi) in enumerate(steps_of(B)):
                    if n >= 2:
                        dve.wait_ge(q.onehot_used, n - 1)
                    bs, shape = slice(lo, hi), (P, 2, hi - lo)

                    def bj(a, width):
                        return a.unsqueeze(3).to_broadcast([*shape, width])

                    def ramp(width):
                        return iota_w[0:P, 0:width].unsqueeze(1).unsqueeze(1).to_broadcast([*shape, width])

                    place = oh_hi[:, n % 2, :, 0:hi - lo, :, :]
                    n_eq = mark(V.tensor_tensor(place[:, :, :, 1, :], ramp(NH), bj(hi_f[:, :, bs], NH), ALU.is_equal))
                    V.tensor_tensor(oh_lo[:, n % 2, :, 0:hi - lo, :], ramp(128), bj(lo_f[:, :, bs], 128),
                                    ALU.is_equal).then_inc(q.onehot, 1)
                    need(n_eq)
                    V.tensor_tensor(place[:, :, :, 0, :], place[:, :, :, 1, :],
                                    node1[k][0:P, bs].unsqueeze(1).unsqueeze(3).to_broadcast([*shape, NH]),
                                    ALU.mult).then_inc(q.onehot, 1)
                    V.tensor_tensor(place[:, :, :, 1, :], place[:, :, :, 1, :], bj(gw[:, :, bs], NH),
                                    ALU.mult).then_inc(q.onehot, 1)
                    if n < 3:
                        aside(f"step{n}")
                dve.wait_ge(q.onehot_used, len(steps_of(B)))
                own(V.scalar_tensor_tensor(out=padz[:, :], in0=ps_m[:, 0:NH], scalar=0.0, in1=pad_row[k][:, :],
                                           op0=ALU.is_equal, op1=ALU.mult))
                V.tensor_copy(slot_w[k][:, 0:NH], ps_m[:, NH:2 * NH])
                V.tensor_scalar(slot_read[k][:, 0:NH], ps_m[:, 0:NH], -1.0, 0.0, ALU.add, ALU.max)
                own(V.scalar_tensor_tensor(out=slot_add[k][:, 0:NH], in0=padz[:, :], scalar=float(s.chunks[0].first - 1),
                                           in1=ps_m[:, 0:NH], op0=ALU.add, op1=ALU.add))
                dve.sem_inc(q.route, 1)

                dve.wait_ge(s_b2, 16)

                def split_tile(n):
                    t = flat(y_hi[:, :, :])
                    dve.wait_ge(q.tile_t, n)
                    V.tensor_copy(t, ps_y[:, :]).then_inc(q.y_hi, 1)
                    dve.wait_ge(q.y_hi, n)
                    V.tensor_tensor(flat(y_lo[:, :, :]), ps_y[:, :], t.bitcast(f32), ALU.subtract).then_inc(q.y_split, 1)

                split_tile(1)
                for e in range(X):
                    nxt = k * X + e + 1
                    first = dve.value_load(starts[k][0:1, e:e + 1], min_val=e, max_val=s.max_tiles - 1)
                    end = dve.value_load(starts[k][0:1, e + 1:e + 2], min_val=e + 1, max_val=s.max_tiles)
                    if k == 0:
                        split_low(nxt, 1)
                    with dve.Fori(first, end) as g:
                        for j in range(NQ):
                            h_in = hf[:, j % 2, :, :]
                            js = slice(2 * j, 2 * j + 2)
                            dve.wait_ge(q.gelu, (g * NQ + j) * 2 + 6)
                            V.tensor_copy(h_hi[:, js, :], h_in).then_inc(q.h_hi, 1)
                            dve.wait_ge(q.h_hi, g * NQ + j + 1)
                            V.tensor_tensor(h_lo[:, js, :], h_in, h_hi[:, js, :].bitcast(f32),
                                            ALU.subtract).then_inc(q.h_split, 1)
                        split_tile(g + 2)
                        if k == 0:
                            pair(g + U0)
                        dve.wait_ge(q.result, g + 1)
                        for h in range(TH):
                            dve.wait_ge(q.added[h], (g + 1) * 16)
                        V.tensor_tensor(ost[:, :, :], ps_o[:, :, 0:D],
                                        b2_bc[:, e, :].unsqueeze(1).to_broadcast([128, TH, D]), ALU.add).then_inc(q.biased, 1)
                        dve.wait_ge(q.biased, g + 2)
                        for h in range(TH):
                            V.tensor_scalar(ost[:, h, :], ost[:, h, :], slot_w[k][:, bass.ds(g * TH + h, 1)], None,
                                            ALU.mult).then_inc(q.staged, 1)
                    if nxt < len(SETS) * X:
                        split_low(nxt, 2)


_INS = ["x", "src", "dst", "edge_weight", "L0_gnn_weight", "L0_gnn_bias", "L0_ffn_Wg", "L0_ffn_bg",
        "L0_ffn_W1", "L0_ffn_b1", "L0_ffn_W2", "L0_ffn_b2"]


def kernel(**inputs):
    import numpy as np
    import concourse.bacc as bacc
    from concourse.bass_utils import run_bass_kernel_spmd

    nc = bacc.Bacc("TRN2", target_bir_lowering=False, num_devices=1)
    arrays, args = {}, []
    for name in _INS:
        a = np.ascontiguousarray(inputs[name])
        arrays[f"in_{name}"] = a
        args.append(nc.dram_tensor(f"in_{name}", a.shape, mybir.dt.from_np(a.dtype), kind="ExternalInput").ap())
    nodes, features = inputs["x"].shape
    args.append(nc.dram_tensor("result", (nodes + PAD_ROWS, features), mybir.dt.float32, kind="ExternalOutput").ap())
    gnn_moe_layer(nc, *args)
    run = run_bass_kernel_spmd(nc, [arrays], core_ids=[0])
    return run.results[0]["result"][:nodes]
```
